# Optimizing a Trainium2 kernel written in Bass

```python
import numpy as np
import jax
import jax.numpy as jnp

def _softmax(x, axis=-1):
    return jax.nn.softmax(x, axis=axis)
def _gelu(x):
    return jax.nn.gelu(x, approximate=True)
def _silu(x):
    return jax.nn.silu(x)
def _sigmoid(x):
    return jax.nn.sigmoid(x)
def _layernorm(x, axis=-1, eps=1e-5):
    m = jnp.mean(x, axis=axis, keepdims=True)
    v = jnp.var(x, axis=axis, keepdims=True)
    return (x - m) / jnp.sqrt(v + eps)
def _scatter_add(tgt, idx, src, axis=0):
    return tgt.at[idx].add(src)
def _segment_sum(src, seg, n):
    return jax.ops.segment_sum(src, seg, n)

kernel_name = 'mk_conv_seq_d2_conv_nchw256_57440d'

def setup_inputs(seed: int = 0):
    np.random.seed(seed)
    _w = jnp.asarray
    def _rec_inputs():
        import jax
        import jax.numpy as jnp
        _gk = jax.random.key(seed)
        x = -0.0002928 + 1 * jax.random.normal(jax.random.fold_in(_gk, 1), (4, 256, 64, 64), jnp.float32)
        return x
    x = _rec_inputs()
    def _L0_conv_setup():
        import jax, jax.numpy as jnp
        import numpy as np
        B, C, W, H = (4, 256, 64, 64)
        D = C // 8
        key = jax.random.key(seed)
        k1, k2, k3, k4, k5 = jax.random.split(key, 5)
        return {'x': jax.random.normal(k1, (B, C, W, H), dtype=jnp.float32), 'q_weight': jax.random.normal(k2, (D, C), dtype=jnp.float32) * 0.05, 'k_weight': jax.random.normal(k3, (D, C), dtype=jnp.float32) * 0.05, 'v_weight': jax.random.normal(k4, (C, C), dtype=jnp.float32) * 0.05, 'gamma': jax.random.normal(k5, (1,), dtype=jnp.float32)}
    _L0_conv_all = _L0_conv_setup()
    _L0_conv_in = {k: v for k, v in _L0_conv_all.items() if k in ('q_weight', 'k_weight', 'v_weight', 'gamma', )}
    del _L0_conv_all

    def _L1_conv_setup():
        import jax, jax.numpy as jnp
        import numpy as np
        key = jax.random.key(seed)
        ks = jax.random.split(key, 6)
        B, C, W, H = (4, 256, 64, 64)
        Ci = C // 8
        s = 0.05
        return {'x': jax.random.normal(ks[0], (B, C, W, H), dtype=jnp.float32), 'wf': jax.random.normal(ks[1], (Ci, C), dtype=jnp.float32) * s, 'bf': jnp.zeros((Ci,), dtype=jnp.float32), 'wg': jax.random.normal(ks[2], (Ci, C), dtype=jnp.float32) * s, 'bg': jnp.zeros((Ci,), dtype=jnp.float32), 'wh': jax.random.normal(ks[3], (Ci, C), dtype=jnp.float32) * s, 'bh': jnp.zeros((Ci,), dtype=jnp.float32), 'wv': jax.random.normal(ks[4], (C, Ci), dtype=jnp.float32) * s, 'bv': jnp.zeros((C,), dtype=jnp.float32), 'gamma': jax.random.normal(ks[5], (1,), dtype=jnp.float32) * 0.1}
    _L1_conv_all = _L1_conv_setup()
    _L1_conv_in = {k: v for k, v in _L1_conv_all.items() if k in ('wf', 'bf', 'wg', 'bg', 'wh', 'bh', 'wv', 'bv', 'gamma', )}
    del _L1_conv_all

    return {
        "x": x,
        "L0_conv_q_weight": _L0_conv_in["q_weight"],
        "L0_conv_k_weight": _L0_conv_in["k_weight"],
        "L0_conv_v_weight": _L0_conv_in["v_weight"],
        "L0_conv_gamma": _L0_conv_in["gamma"],
        "L1_conv_wf": _L1_conv_in["wf"],
        "L1_conv_bf": _L1_conv_in["bf"],
        "L1_conv_wg": _L1_conv_in["wg"],
        "L1_conv_bg": _L1_conv_in["bg"],
        "L1_conv_wh": _L1_conv_in["wh"],
        "L1_conv_bh": _L1_conv_in["bh"],
        "L1_conv_wv": _L1_conv_in["wv"],
        "L1_conv_bv": _L1_conv_in["bv"],
        "L1_conv_gamma": _L1_conv_in["gamma"],
    }

def reference(x, L0_conv_q_weight, L0_conv_k_weight, L0_conv_v_weight, L0_conv_gamma, L1_conv_wf, L1_conv_bf, L1_conv_wg, L1_conv_bg, L1_conv_wh, L1_conv_bh, L1_conv_wv, L1_conv_bv, L1_conv_gamma):
    import jax
    import jax.numpy as jnp
    def _L0_conv_ref(x, q_weight, k_weight, v_weight, gamma):
        import jax, jax.numpy as jnp
        import numpy as np
        B, C, W, H = (4, 256, 64, 64)
        D = C // 8
        b, c, w, h = x.shape
        n = w * h
        xf = x.reshape(b, c, n)
        q = jnp.einsum('dc,bcn->bdn', q_weight, xf)
        k = jnp.einsum('dc,bcn->bdn', k_weight, xf)
        v = jnp.einsum('oc,bcn->bon', v_weight, xf)
        energy = jnp.einsum('bdi,bdj->bij', q, k)
        attn = jax.nn.softmax(energy, axis=-1)
        out = jnp.einsum('bcj,bij->bci', v, attn)
        out = out.reshape(b, c, w, h)
        return gamma[0] * out + x

    def _L1_conv_ref(x, wf, bf, wg, bg, wh, bh, wv, bv, gamma):
        import jax, jax.numpy as jnp
        import numpy as np
        B, C, W, H = x.shape
        N = W * H
        xf = x.reshape(B, C, N)
        f = jnp.einsum('bcn,oc->bon', xf, wf) + bf[:, None]
        g = jnp.einsum('bcn,oc->bon', xf, wg) + bg[:, None]
        h = jnp.einsum('bcn,oc->bon', xf, wh) + bh[:, None]
        logits = jnp.einsum('bcq,bck->bqk', f, g)
        attn = jax.nn.softmax(logits, axis=-1)
        x0 = jnp.einsum('bck,bqk->bcq', h, attn)
        v = jnp.einsum('bcn,oc->bon', x0, wv) + bv[:, None]
        v = v.reshape(B, C, W, H)
        return v * gamma[0] + x

    def _gn(v, G=32, eps=1e-5):
        B_, C_, H_, W_ = v.shape
        g = v.reshape(B_, G, C_ // G, H_, W_)
        m = jnp.mean(g, axis=(2, 3, 4), keepdims=True)
        s = jnp.var(g, axis=(2, 3, 4), keepdims=True)
        return ((g - m) / jnp.sqrt(s + eps)).reshape(v.shape)

    def _ln_c(v, eps=1e-6):
        m = jnp.mean(v, axis=1, keepdims=True)
        s = jnp.var(v, axis=1, keepdims=True)
        return (v - m) / jnp.sqrt(s + eps)

    def _ln_t(v, eps=1e-5):
        m = jnp.mean(v, axis=-1, keepdims=True)
        s = jnp.var(v, axis=-1, keepdims=True)
        return (v - m) / jnp.sqrt(s + eps)

    def _to_tokens(v):
        B_, C_, H_, W_ = v.shape
        return v.reshape(B_, C_, H_ * W_).transpose(0, 2, 1)
    def _from_tokens(t, like):
        B_, C_, H_, W_ = like.shape
        return t.transpose(0, 2, 1).reshape(B_, C_, H_, W_)

    x = _L0_conv_ref(x, L0_conv_q_weight, L0_conv_k_weight, L0_conv_v_weight, L0_conv_gamma)
    x = _L1_conv_ref(x, L1_conv_wf, L1_conv_bf, L1_conv_wg, L1_conv_bg, L1_conv_wh, L1_conv_bh, L1_conv_wv, L1_conv_bv, L1_conv_gamma)
    return x


_drawn_inputs = setup_inputs


def setup_inputs(seed=0):
    import zlib

    import numpy as np

    out = dict(_drawn_inputs(seed))
    spreads = {'L1_conv_bf': (0.0, 0.8),
     'L1_conv_bg': (0.0, 0.8),
     'L1_conv_bh': (0.0, 0.8),
     'L1_conv_bv': (0.0, 0.8)}
    factors = {'L1_conv_wf': 6.906, 'L1_conv_wg': 6.792, 'L1_conv_wh': 6.804, 'L1_conv_wv': 6.628}
    for name, (base, spread) in spreads.items():
        noise = np.random.default_rng([zlib.crc32(name.encode()), seed]).standard_normal(out[name].shape)
        drawn = base * np.exp(spread * noise) if base else spread * noise
        out[name] = jnp.asarray(drawn.astype(out[name].dtype))
    for name, factor in factors.items():
        out[name] = (out[name] * factor).astype(out[name].dtype)
    return out
```

```python
from contextlib import ExitStack

import concourse.bass as bass
from concourse import mybir

F32 = mybir.dt.float32
F32R = mybir.dt.float32r
ALU = mybir.AluOpType
ACT = mybir.ActivationFunctionType
AX = mybir.AxisListType

P = 128
BATCH, C, N, D = 4, 256, 64 * 64, 32
CT = C // P
KT = N // P
QB = 512
NBLK = N // QB
SUB = QB // P
CHUNK = QB
NCH = N // CHUNK
STACK = 3 * D
MAXROW = STACK
KROWS = STACK + 2
HW = 2 * D + 1
RING = 4
AHEAD = 3
SPLIT_AHEAD = 2
PRIMED = 1
MXSTEPS = 26
LATE = 3
HI_ON_ACT = [lambda j: j % 2 == 0, lambda j: True]


def row_tiles(step):
    return [u for u in range(SUB * NCH) if u * MXSTEPS // (SUB * NCH) == step]


def last_row_step(s):
    return (NCH * s + NCH - 1) * MXSTEPS // (SUB * NCH)


def hi_count(layer, on_act, j):
    return sum(1 for t in range(j + 1) if HI_ON_ACT[layer](t % KT) == on_act)


def build(nc, x, wqk, wv, wh, wo, gamma, b_fg, b_h, b_o, out):
    nc.disable_value_cache = True
    with ExitStack() as ctx:
        def sb(name, shape, dt=F32):
            return ctx.enter_context(nc.sbuf_tensor(name, shape, dt))

        def bank(name):
            return ctx.enter_context(nc.psum_tensor(name, [P, QB], F32))

        def sem(name):
            return ctx.enter_context(nc.semaphore(name))

        def sems(name):
            return [sem(f"{name}{layer}") for layer in range(2)]

        x_sb = sb("x_sb", [P, CT, N])
        qs = sb("q_stack", [P, N], F32R)
        ks = sb("k_stack", [P, N], F32R)
        q_now = sb("q_now", [STACK, SUB, P], F32R)
        v_hi = sb("v_hi", [P, KT, C], F32R)
        v_lo = sb("v_lo", [P, KT, C], F32R)
        h_f = sb("h_f", [P, KT, D])
        h_st = sb("h_st", [P, KT, HW], F32R)
        e_t = sb("e_t", [P, RING, QB])
        p_hi = sb("p_hi", [P, RING, QB], F32R)
        p_lo = sb("p_lo", [P, RING, QB], F32R)
        r_all = sb("r_all", [P, QB])
        o_t = sb("o_t", [P, CT, QB])
        xs = sb("xs", [HW, QB])
        xt = sb("xt", [P, SUB, HW])
        xn = sb("xn", [P, SUB, D])
        x0n = sb("x0n", [D, QB])
        negmax = sb("negmax", [P, SUB, NCH])
        lpart = sb("lpart", [P, SUB, NCH])
        wgt = sb("wgt", [P, SUB, NCH])
        wl = sb("wl", [P, SUB, NCH])
        nm = sb("nm", [P, SUB])
        nm_cols = sb("nm_cols", [P, SUB, KROWS], F32R)
        lsum = sb("lsum", [P, SUB])
        linv = sb("linv", [P, SUB])
        r_col = sb("r_col", [P, SUB])
        l1inv = sb("l1inv", [P, SUB])
        l1r = sb("l1r", [P, SUB])
        ident = sb("ident", [P, P])
        wqk_sb = sb("wqk_sb", [P, 2, CT, 2, STACK])
        wv_sb = sb("wv_sb", [P, CT, C])
        wh_sb = sb("wh_sb", [P, CT, D])
        wo_sb = sb("wo_sb", [D, C])
        gam = sb("gam", [P, 2])
        bqk = sb("bqk", [STACK, 2, 2])
        bh_sb = sb("bh_sb", [P, D])
        bo_sb = sb("bo_sb", [P, CT])
        gbo = sb("gbo", [P, CT])

        st = [bank("st0"), bank("st1")]
        mx = [bank("mx0"), bank("mx1")]
        acc = [bank("acc0"), bank("acc1")]
        aux_m = bank("aux_m")
        aux_r = bank("aux_r")
        proj = [mx[0], mx[1], st[0], st[1]]

        w_in, zeroed, ident_ok, gbo_ok = sem("w_in"), sem("zeroed"), sem("ident_ok"), sem("gbo_ok")
        x_in, out_done = sem("x_in"), sem("out_done")
        qk_psum, qk_hi, qk_lo = sems("qk_psum"), sems("qk_hi"), sems("qk_lo")
        v_psum, v_hi_ok, v_ok = sems("v_psum"), sems("v_hi_ok"), sems("v_ok")
        hf_ok = sem("hf_ok")
        q_now_ok = sems("q_now_ok")
        rows_psum, rowmax_ok, rowsum_ok = sems("rows_psum"), sems("rowmax_ok"), sem("rowsum_ok")
        nm_step, nm_rowpsum, nm_rows = sems("nm_step"), sems("nm_rowpsum"), sems("nm_rows")
        wgt_ok, l_step = sem("wgt_ok"), sem("l_step")
        st_psum, exp_ok = sems("st_psum"), sems("exp_ok")
        hi_act, hi_dve, lo_ok = sems("hi_act"), sems("hi_dve"), sems("lo_ok")
        pv_done, acc0_done = sems("pv_done"), sem("acc0_done")
        r_psum, r_ok = sem("r_psum"), sem("r_ok")
        evac, y_ok = [sem("evac_c0"), sem("evac_c1")], sem("y_ok")
        xs_ok, xt_psum, xt_ok, ep_step = sem("xs_ok"), sem("xt_psum"), sem("xt_ok"), sem("ep_step")
        x0_psum, x0_ok, o_psum, o_ok = sem("x0_psum"), sem("x0_ok"), sem("o_psum"), sem("o_ok")

        block = ctx.enter_context(nc.Block())


        def cols(ib, at=0, n=QB):
            return bass.ds(ib * QB + at, n)

        def blocks(eng, body, first_differs):
            if first_differs:
                body(0, True, False)
            with_first = 1 if first_differs else 0
            with eng.Fori(with_first, NBLK - 1) as ib:
                body(ib, False, False)
            body(NBLK - 1, False, True)

        @block.sync
        def _(eng):
            eng.sem_inc(out_done, PRIMED)

            def load(b, ib):
                eng.dma_start(x_sb[:, :, cols(ib)],
                              x[b].rearrange("(k p) n -> p k n", p=P)[:, :, cols(ib)]).then_inc(x_in, 16)

            def store(b, ib):
                eng.wait_ge(o_ok, (b * NBLK + ib) * 2 + 2)
                eng.dma_start(out[b].rearrange("(k p) n -> p k n", p=P)[:, :, cols(ib)],
                              o_t[:, :, :]).then_inc(out_done, 16)

            for sbuf, dram in ((wqk_sb[:, :, :, :, :], wqk), (wv_sb[:, :, :], wv), (wh_sb[:, :, :], wh),
                               (wo_sb[:, :], wo), (gam[:, :], gamma), (bh_sb[:, :], b_h),
                               (bo_sb[:, :], b_o), (bqk[:, 1, :], b_fg)):
                eng.dma_start(sbuf, dram).then_inc(w_in, 16)
            for ib in range(NBLK):
                load(0, ib)
            for b in range(BATCH):
                with eng.Fori(0, NBLK) as ib:
                    store(b, ib)
                    if b < BATCH - 1:
                        load(b + 1, ib)
            eng.wait_ge(out_done, PRIMED + 16 * BATCH * NBLK)

        @block.gpsimd
        def _(eng):
            eng.sem_inc(y_ok, PRIMED)
            eng.memset(ident[:, :], 0.0).then_inc(ident_ok, 1)
            eng.wait_ge(ident_ok, 1)
            eng.affine_select(out=ident[:, :], in_=ident[:, :], compare_op=ALU.not_equal, fill=1.0,
                              base=0, pattern=[[-1, P]], channel_multiplier=1).then_inc(ident_ok, 1)

            def fills(g, ib, layer):
                for s in range(SUB):
                    eng.wait_ge(rows_psum[layer], (g + 1) * SUB * NCH + NCH * (s + 1))
                    eng.tensor_copy(q_now[:, s, :], qs[0:STACK, cols(ib + 2, s * P, P)])\
                       .then_inc(q_now_ok[layer], 1)

            def residual(g, ib):
                for c in range(CT):
                    eng.wait_ge(evac[c], PRIMED + g + 1)
                    ins = eng.tensor_tensor(x_sb[:, c, cols(ib)], x_sb[:, c, cols(ib)], o_t[:, c, :], ALU.add)
                ins.then_inc(y_ok, 1)

            with eng.Fori(0, BATCH) as b:
                for layer in range(2):
                    g0 = b * NBLK
                    with eng.Fori(0, NBLK - 2) as ib:
                        fills(g0 + ib, ib, layer)
                        if layer == 0:
                            residual(g0 + ib, ib)
                    if layer == 0:
                        for ib in (NBLK - 2, NBLK - 1):
                            residual(g0 + ib, ib)

        @block.tensor
        def _(eng):
            def project_qk(g0, layer):
                for n in range(NBLK):
                    for r in range(2):
                        i = 2 * n + r
                        if i >= len(proj):
                            eng.wait_ge(qk_lo[layer], 2 * g0 + i + 1 - len(proj))
                        for k in range(CT):
                            mm = eng.matmul(proj[i % 4][0:STACK, :], wqk_sb[:, layer, k, r, :],
                                            x_sb[:, k, n * QB:(n + 1) * QB], start=(k == 0), stop=(k == 1))
                        mm.then_inc(qk_psum[layer], 1)

            def project_v(g0, pair):
                if pair >= 2:
                    eng.wait_ge(v_ok[0], 2 * g0 + pair - 1)
                for i in range(2):
                    t = 2 * pair + i
                    for k in range(CT):
                        mm = eng.matmul(acc[pair % 2][:, i * C:(i + 1) * C], x_sb[:, k, t * P:(t + 1) * P],
                                        wv_sb[:, k, :], start=(i == 0 and k == 0), stop=(i == 1 and k == 1),
                                        skip_group_check=True)
                mm.then_inc(v_psum[0], 1)

            def project_h(g0, t):
                half, i = divmod(t, KT // 2)
                for k in range(CT):
                    mm = eng.matmul([acc[1], aux_r][half][:, i * D:(i + 1) * D], x_sb[:, k, t * P:(t + 1) * P],
                                    wh_sb[:, k, :], start=(i == 0 and k == 0), stop=(i == KT // 2 - 1 and k == 1),
                                    skip_group_check=True)
                if i == KT // 2 - 1:
                    mm.then_inc(v_psum[1], 1)

            def rows(g, u, layer, free):
                s, c = divmod(u, NCH)
                if free:
                    used = rowsum_ok if layer == 0 else rowmax_ok[1]
                    eng.wait_ge(used, g * SUB * NCH + u - 1)
                if c == 0:
                    eng.wait_ge(q_now_ok[layer], g * SUB + s + 1)
                eng.matmul(mx[u % 2][:, :], q_now[:, s, :], ks[0:STACK, c * CHUNK:(c + 1) * CHUNK],
                           start=True, stop=True).then_inc(rows_psum[layer], 1)

            def max_rows(g, s, layer, free):
                eng.wait_ge(nm_step[layer], 3 * (g * SUB + s + 1))
                if free:
                    eng.wait_ge(nm_rows[layer], g * SUB + s)
                eng.transpose(aux_m[0:KROWS, s * P:(s + 1) * P], nm_cols[:, s, :].bitcast(F32),
                              ident[:, :]).then_inc(nm_rowpsum[layer], 1)

            def factor_rows(g):
                eng.wait_ge(l_step, 4 * (g * SUB + SUB))
                eng.wait_ge(r_ok, PRIMED + g)
                for s in range(SUB):
                    mm = eng.transpose(aux_r[:, s * P:(s + 1) * P], r_col[:, s:s + 1].to_broadcast([P, P]),
                                       ident[:, :])
                mm.then_inc(r_psum, 1)

            def scores_t(g, ib, j, layer, free):
                if j % KT == 0:
                    eng.wait_ge(nm_rows[layer], (g + j // KT) * SUB + SUB)
                if free:
                    eng.wait_ge(exp_ok[layer], g * KT + j - 1)
                eng.matmul(st[j % 2][:, :], ks[0:KROWS, (j % KT) * P:(j % KT + 1) * P],
                           qs[0:KROWS, cols(ib + j // KT)], start=True, stop=True).then_inc(st_psum[layer], 1)

            def sums0(g, j):
                eng.wait_ge(lo_ok[0], PRIMED + g * KT + j + 1)
                a, b = p_hi[:, j % RING, :], p_lo[:, j % RING, :]
                for c in range(CT):
                    hi, lo = v_hi[:, j, c * P:(c + 1) * P], v_lo[:, j, c * P:(c + 1) * P]
                    if j == 0:
                        eng.wait_ge(evac[c], PRIMED + g)
                    eng.matmul(acc[c][:, :], hi, a, start=(j == 0), stop=False)
                    eng.matmul(acc[c][:, :], lo, a, start=False, stop=False)
                    mm = eng.matmul(acc[c][:, :], hi, b, start=False, stop=(j == KT - 1))
                    if c == 0 and j == KT - 1:
                        mm.then_inc(acc0_done, 1)
                mm.then_inc(pv_done[0], 1)

            def sums1(g, j):
                eng.wait_ge(lo_ok[1], PRIMED + g * KT + j + 1)
                if j == 0:
                    eng.wait_ge(xs_ok, PRIMED + g)
                eng.matmul(acc[0][0:HW, :], h_st[:, j, :], p_hi[:, j % RING, :], start=(j == 0), stop=False)
                eng.matmul(acc[0][0:HW, :], h_st[:, j, :], p_lo[:, j % RING, :], start=False,
                           stop=(j == KT - 1)).then_inc(pv_done[1], 1)

            def turn_sums(g):
                eng.wait_ge(xs_ok, PRIMED + g + 1)
                for s in range(SUB):
                    mm = eng.transpose(aux_r[:, s * HW:(s + 1) * HW], xs[:, s * P:(s + 1) * P], ident[0:HW, 0:HW])
                mm.then_inc(xt_psum, 1)

            def turn_back(g):
                eng.wait_ge(ep_step, 4 * g + 4)
                for s in range(SUB):
                    mm = eng.transpose(aux_r[0:D, s * P:(s + 1) * P], xn[:, s, :], ident[:, :])
                mm.then_inc(x0_psum, 1)

            def widen(g):
                eng.wait_ge(x0_ok, g + 1)
                for c, to in enumerate((acc[1], aux_r)):
                    eng.matmul(to[:, :], wo_sb[:, c * P:(c + 1) * P], x0n[:, :], start=True, stop=True)\
                       .then_inc(o_psum, 1)

            for done in pv_done:
                eng.sem_inc(done, PRIMED)
            eng.wait_ge(w_in, 16 * 8)
            eng.wait_ge(ident_ok, 2)
            eng.wait_ge(zeroed, 4)
            with eng.Fori(0, BATCH) as b:
                for layer in range(2):
                    g0 = b * NBLK
                    if layer == 0:
                        eng.wait_ge(x_in, 16 * NBLK * (b + 1))
                    else:
                        eng.wait_ge(y_ok, PRIMED + g0 + NBLK)
                    project_qk(g0, layer)
                    eng.wait_ge(qk_lo[layer], 2 * g0 + 2 * NBLK)
                    for u in range(SUB * NCH):
                        if layer == 0 and u % 2 == 0:
                            project_v(g0, u // 2)
                        if layer == 1:
                            project_h(g0, u)
                        rows(g0, u, layer, u >= 2)
                        if u % NCH == 4 and u > NCH:
                            max_rows(g0, u // NCH - 1, layer, u // NCH > 1)
                    max_rows(g0, SUB - 1, layer, True)
                    for j in range(AHEAD - 1):
                        scores_t(g0, 0, j, layer, j >= 2)
                    eng.wait_ge(v_ok[layer], 2 * g0 + 2 * NBLK if layer == 0 else 2 * b + 2)
                    scores_t(g0, 0, AHEAD - 1, layer, True)

                    def body(ib, first, last):
                        g = g0 + ib
                        for j in range(KT):
                            if not last or j + AHEAD < KT:
                                scores_t(g, ib, j + AHEAD, layer, True)
                            if not last:
                                for u in row_tiles(j):
                                    rows(g + 1, u, layer, True)
                                for s in range(SUB):
                                    if j == last_row_step(s) + LATE:
                                        max_rows(g + 1, s, layer, True)
                            if layer == 0:
                                if j == 3:
                                    factor_rows(g)
                                sums0(g, j)
                            else:
                                if not first and j == 2:
                                    turn_sums(g - 1)
                                if not first and j == 6:
                                    turn_back(g - 1)
                                if not first and j == 9:
                                    widen(g - 1)
                                sums1(g, j)

                    blocks(eng, body, layer == 1)
                    if layer == 1:
                        turn_sums(g0 + NBLK - 1)
                        turn_back(g0 + NBLK - 1)
                        widen(g0 + NBLK - 1)

        @block.scalar
        def _(eng):
            def stack_hi(g0, layer):
                for n in range(NBLK):
                    for r, to in enumerate((qs, ks)):
                        i = 2 * n + r
                        eng.wait_ge(qk_psum[layer], 2 * g0 + i + 1)
                        eng.activation(to[0:STACK, n * QB:(n + 1) * QB], proj[i % 4][0:STACK, :], ACT.Identity,
                                       bias=bqk[:, layer, r:r + 1]).then_inc(qk_hi[layer], 1)

            def first_queries(g, blk, s, layer):
                if blk:
                    eng.wait_ge(rows_psum[layer], g * SUB * NCH + NCH * (s + 1))
                else:
                    eng.wait_ge(qk_lo[layer], (g + NBLK) * 2)
                eng.activation(q_now[:, s, :], 
                               qs[0:STACK, blk * QB + s * P:blk * QB + (s + 1) * P].bitcast(F32), ACT.Copy)\
                   .then_inc(q_now_ok[layer], 1)

            def rowsum(g, u):
                s, c = divmod(u, NCH)
                eng.wait_ge(rowmax_ok[0], g * SUB * NCH + u + 1)
                eng.activation(mx[u % 2][:, :], mx[u % 2][:, :], ACT.Exp, bias=negmax[:, s, c:c + 1],
                               accum_out=lpart[:, s, c:c + 1]).then_inc(rowsum_ok, 1)

            def weights(g, s):
                eng.wait_ge(nm_step[0], 3 * (g * SUB + s) + 1)
                eng.activation(wgt[:, s, :], negmax[:, s, :], ACT.Exp, scale=-1.0,
                               bias=nm[:, s:s + 1]).then_inc(wgt_ok, 1)

            def put_max_rows(g, blk, s, layer):
                eng.wait_ge(nm_rowpsum[layer], g * SUB + s + 1)
                eng.activation(qs[MAXROW:KROWS, cols(blk, s * P, P)], aux_m[MAXROW:KROWS, s * P:(s + 1) * P],
                               ACT.Copy).then_inc(nm_rows[layer], 1)

            def exps(g, j, layer, free):
                eng.wait_ge(st_psum[layer], g * KT + j + 1)
                if free:
                    eng.wait_ge(lo_ok[layer], PRIMED + g * KT + j + 1 - RING)
                eng.activation(e_t[:, j % RING, :], st[j % 2][:, :], ACT.Exp).then_inc(exp_ok[layer], 1)

            def hi(g, j, layer, free):
                if not HI_ON_ACT[layer](j % KT):
                    return
                eng.wait_ge(exp_ok[layer], g * KT + j + 1)
                if free:
                    eng.wait_ge(pv_done[layer], PRIMED + g * KT + j + 1 - RING)
                eng.activation(p_hi[:, j % RING, :], e_t[:, j % RING, :], ACT.Copy).then_inc(hi_act[layer], 1)

            def put_factors(g):
                eng.wait_ge(r_psum, g + 1)
                eng.wait_ge(evac[1], PRIMED + g)
                eng.activation(r_all[:, :], aux_r[:, :], ACT.Copy).then_inc(r_ok, 1)

            for done in (r_ok, xs_ok):
                eng.sem_inc(done, PRIMED)
            eng.wait_ge(w_in, 16 * 8)
            eng.wait_ge(zeroed, 4)
            with eng.Fori(0, BATCH) as b:
                for layer in range(2):
                    g0 = b * NBLK
                    stack_hi(g0, layer)
                    for s in range(SUB):
                        first_queries(g0, 0, s, layer)
                    for u in range(SUB * NCH):
                        if layer == 0:
                            if u % 2 == 0:
                                pair = u // 2
                                eng.wait_ge(v_psum[0], 2 * g0 + pair + 1)
                                eng.activation(v_hi[:, 2 * pair:2 * pair + 2, :], acc[pair % 2][:, :], ACT.Copy)\
                                   .then_inc(v_hi_ok[0], 1)
                            rowsum(g0, u)
                            if u % NCH == NCH - 1:
                                weights(g0, u // NCH)
                        if u % NCH == NCH - 1:
                            first_queries(g0, 1, u // NCH, layer)
                        if u % NCH == 5 and u > NCH:
                            put_max_rows(g0, 0, u // NCH - 1, layer)
                    put_max_rows(g0, 0, SUB - 1, layer)
                    if layer == 1:
                        for half in range(2):
                            t = slice(half * KT // 2, (half + 1) * KT // 2)
                            eng.wait_ge(hf_ok, 2 * b + half + 1)
                            eng.activation(h_st[:, t, 0:D], h_f[:, t, :], ACT.Copy).then_inc(v_hi_ok[1], 1)
                    for j in range(AHEAD):
                        exps(g0, j, layer, False)
                    for j in range(SPLIT_AHEAD):
                        hi(g0, j, layer, False)

                    def body(ib, first, last):
                        g = g0 + ib
                        for j in range(KT):
                            if not last or j + AHEAD < KT:
                                exps(g, j + AHEAD, layer, True)
                            if not last or j + SPLIT_AHEAD < KT:
                                hi(g, j + SPLIT_AHEAD, layer, True)
                            if not last:
                                if layer == 0:
                                    for u in row_tiles(j):
                                        rowsum(g + 1, u)
                                        if u % NCH == NCH - 1:
                                            weights(g + 1, u // NCH)
                                for s in range(SUB):
                                    if j == last_row_step(s) + LATE:
                                        put_max_rows(g + 1, ib + 1, s, layer)
                            if layer == 0 and j == 4:
                                put_factors(g)
                            if layer == 1 and not first and j == 3:
                                take_turned(g - 1)
                            if layer == 1 and not first and j == 7:
                                take_back(g - 1)
                        if layer == 1:
                            eng.wait_ge(pv_done[1], PRIMED + g * KT + KT)
                            eng.activation(xs[:, :], acc[0][0:HW, :], ACT.Copy).then_inc(xs_ok, 1)

                    def take_turned(g):
                        eng.wait_ge(xt_psum, g + 1)
                        eng.activation(xt[:, :, :], aux_r[:, 0:SUB * HW], ACT.Copy).then_inc(xt_ok, 1)

                    def take_back(g):
                        eng.wait_ge(x0_psum, g + 1)
                        eng.activation(x0n[:, :], aux_r[0:D, :], ACT.Copy).then_inc(x0_ok, 1)

                    blocks(eng, body, layer == 1)
                    if layer == 1:
                        take_turned(g0 + NBLK - 1)
                        take_back(g0 + NBLK - 1)

        @block.vector
        def _(eng):
            def stack_lo(g0, layer):
                for n in range(NBLK):
                    for r, (to, at) in enumerate(((qs, D), (ks, 2 * D))):
                        i = 2 * n + r
                        eng.wait_ge(qk_hi[layer], 2 * g0 + i + 1)
                        part = to[at:at + D, n * QB:(n + 1) * QB]
                        eng.scalar_tensor_tensor(part, proj[i % 4][at:at + D, :], bqk[at:at + D, layer, r:r + 1],
                                                 part.bitcast(F32), ALU.add, ALU.subtract)\
                           .then_inc(qk_lo[layer], 1)

            def rowmax(g, u, layer):
                s, c = divmod(u, NCH)
                eng.wait_ge(rows_psum[layer], g * SUB * NCH + u + 1)
                eng.tensor_reduce(negmax[:, s, c:c + 1], mx[u % 2][:, :], AX.X, ALU.max, negate=True)\
                   .then_inc(rowmax_ok[layer], 1)
                if c == NCH - 1:
                    done = 3 * (g * SUB + s)
                    eng.wait_ge(rowmax_ok[layer], g * SUB * NCH + u + 1)
                    eng.tensor_reduce(nm[:, s:s + 1], negmax[:, s, :], AX.X, ALU.min).then_inc(nm_step[layer], 1)
                    eng.wait_ge(nm_step[layer], done + 1)
                    eng.tensor_copy(nm_cols[:, s, MAXROW:MAXROW + 1], nm[:, s:s + 1]).then_inc(nm_step[layer], 1)
                    eng.wait_ge(nm_step[layer], done + 2)
                    eng.tensor_tensor(nm_cols[:, s, MAXROW + 1:KROWS], nm[:, s:s + 1], nm_cols[:, s, MAXROW:MAXROW + 1].bitcast(F32),
                                      ALU.subtract).then_inc(nm_step[layer], 1)

            def factor(g, s, free):
                done = 4 * (g * SUB + s)
                eng.wait_ge(wgt_ok, g * SUB + s + 1)
                eng.tensor_tensor(wl[:, s, :], wgt[:, s, :], lpart[:, s, :], ALU.mult).then_inc(l_step, 1)
                eng.wait_ge(l_step, done + 1)
                eng.tensor_reduce(lsum[:, s:s + 1], wl[:, s, :], AX.X, ALU.add).then_inc(l_step, 1)
                eng.wait_ge(l_step, done + 2)
                eng.reciprocal(linv[:, s:s + 1], lsum[:, s:s + 1]).then_inc(l_step, 1)
                eng.wait_ge(l_step, done + 3)
                if free:
                    eng.wait_ge(r_psum, g)
                eng.tensor_scalar(r_col[:, s:s + 1], linv[:, s:s + 1], gam[:, 0:1], None, ALU.mult)\
                   .then_inc(l_step, 1)

            def split(g, j, layer, free):
                e, h = e_t[:, j % RING, :], p_hi[:, j % RING, :]
                per = sum(1 for t in range(KT) if HI_ON_ACT[layer](t))
                if HI_ON_ACT[layer](j % KT):
                    eng.wait_ge(hi_act[layer], g * per + hi_count(layer, True, j))
                    if free:
                        eng.wait_ge(pv_done[layer], PRIMED + g * KT + j + 1 - RING)
                else:
                    eng.wait_ge(exp_ok[layer], g * KT + j + 1)
                    if free:
                        eng.wait_ge(pv_done[layer], PRIMED + g * KT + j + 1 - RING)
                    eng.tensor_copy(h, e).then_inc(hi_dve[layer], 1)
                    eng.wait_ge(hi_dve[layer], g * (KT - per) + hi_count(layer, False, j))
                eng.tensor_tensor(p_lo[:, j % RING, :], e, h.bitcast(F32), ALU.subtract).then_inc(lo_ok[layer], 1)

            def take_sums(g):
                eng.wait_ge(r_ok, PRIMED + g + 1)
                for c in range(CT):
                    if c == 0:
                        eng.wait_ge(acc0_done, g + 1)
                        eng.wait_ge(y_ok, PRIMED + g)
                    else:
                        eng.wait_ge(pv_done[0], PRIMED + g * KT + KT)
                    eng.tensor_tensor(o_t[:, c, :], acc[c][:, :], r_all[:, :], ALU.mult).then_inc(evac[c], 1)

            def normalise(g):
                eng.wait_ge(xt_ok, g + 1)
                eng.reciprocal(l1inv[:, :], xt[:, :, 2 * D:HW]).then_inc(ep_step, 1)
                eng.tensor_tensor(xt[:, :, 0:D], xt[:, :, 0:D], xt[:, :, D:2 * D], ALU.add).then_inc(ep_step, 1)
                eng.wait_ge(ep_step, 4 * g + 2)
                eng.tensor_scalar(l1r[:, :], l1inv[:, :], gam[:, 1:2], None, ALU.mult).then_inc(ep_step, 1)
                eng.wait_ge(ep_step, 4 * g + 3)
                eng.tensor_tensor(xn[:, :, :], xt[:, :, 0:D],
                                  l1r[:, :].rearrange("p (s a) -> p s a", a=1).to_broadcast([P, SUB, D]),
                                  ALU.mult).then_inc(ep_step, 1)

            def finish(g, ib):
                eng.wait_ge(out_done, PRIMED + 16 * g)
                for c, at in enumerate((acc[1], aux_r)):
                    eng.wait_ge(o_psum, 2 * g + c + 1)
                    eng.scalar_tensor_tensor(o_t[:, c, :], at[:, :], gbo[:, c:c + 1], x_sb[:, c, cols(ib)],
                                             ALU.add, ALU.add).then_inc(o_ok, 1)

            for done in (*lo_ok, *evac):
                eng.sem_inc(done, PRIMED)
            eng.memset(bqk[:, 0, :], 0.0).then_inc(zeroed, 1)
            eng.memset(ks[MAXROW:KROWS, :].bitcast(F32), 1.0).then_inc(zeroed, 1)
            eng.memset(h_st[:, :, 2 * D:HW].bitcast(F32), 1.0).then_inc(zeroed, 1)
            eng.memset(nm_cols[:, :, :].bitcast(F32), 0.0).then_inc(zeroed, 1)
            eng.wait_ge(w_in, 16 * 8)
            eng.wait_ge(zeroed, 4)
            eng.tensor_scalar(gbo[:, :], bo_sb[:, :], gam[:, 1:2], None, ALU.mult).then_inc(gbo_ok, 1)
            eng.wait_ge(gbo_ok, 1)
            with eng.Fori(0, BATCH) as b:
                for layer in range(2):
                    g0 = b * NBLK
                    stack_lo(g0, layer)
                    for u in range(SUB * NCH):
                        rowmax(g0, u, layer)
                        if layer == 0 and u % 2 == 0:
                            pair = u // 2
                            eng.wait_ge(v_hi_ok[0], 2 * g0 + pair + 1)
                            part = v_hi[:, 2 * pair:2 * pair + 2, :].bitcast(F32)
                            eng.tensor_tensor(v_lo[:, 2 * pair:2 * pair + 2, :],
                                              acc[pair % 2][:, :].rearrange("p (t c) -> p t c", t=2), part,
                                              ALU.subtract).then_inc(v_ok[0], 1)
                        if layer == 0 and u % NCH == 4 and u > NCH:
                            factor(g0, u // NCH - 1, False)
                    if layer == 0:
                        factor(g0, SUB - 1, False)
                    else:
                        for half, at in enumerate((acc[1], aux_r)):
                            t = slice(half * KT // 2, (half + 1) * KT // 2)
                            eng.wait_ge(v_psum[1], 2 * b + half + 1)
                            eng.tensor_tensor(h_f[:, t, :], at[:, :].rearrange("p (t d) -> p t d", d=D),
                                              bh_sb[:, :].rearrange("p (a d) -> p a d", a=1)
                                              .to_broadcast([P, KT // 2, D]), ALU.add).then_inc(hf_ok, 1)
                        for half in range(2):
                            t = slice(half * KT // 2, (half + 1) * KT // 2)
                            eng.wait_ge(v_hi_ok[1], 2 * b + half + 1)
                            eng.tensor_tensor(h_st[:, t, D:2 * D], h_f[:, t, :], h_st[:, t, 0:D].bitcast(F32),
                                              ALU.subtract).then_inc(v_ok[1], 1)
                    for j in range(SPLIT_AHEAD):
                        split(g0, j, layer, False)

                    def body(ib, first, last):
                        g = g0 + ib
                        for j in range(KT):
                            if not last:
                                for u in row_tiles(j):
                                    rowmax(g + 1, u, layer)
                                if layer == 0:
                                    for s in range(SUB):
                                        if j == last_row_step(s) + LATE:
                                            factor(g + 1, s, True)
                            if not last or j + SPLIT_AHEAD < KT:
                                split(g, j + SPLIT_AHEAD, layer, True)
                            if layer == 1 and not first and j == 4:
                                normalise(g - 1)
                            if layer == 1 and not first and j == 10:
                                finish(g - 1, ib - 1)
                        if layer == 0:
                            take_sums(g)

                    blocks(eng, body, layer == 1)
                    if layer == 1:
                        normalise(g0 + NBLK - 1)
                        finish(g0 + NBLK - 1, NBLK - 1)


def kernel(x, L0_conv_q_weight, L0_conv_k_weight, L0_conv_v_weight, L0_conv_gamma,
           L1_conv_wf, L1_conv_bf, L1_conv_wg, L1_conv_bg, L1_conv_wh, L1_conv_bh,
           L1_conv_wv, L1_conv_bv, L1_conv_gamma):
    import numpy as np
    from concourse import bacc
    from concourse.bass_utils import run_bass_kernel_spmd

    x = np.asarray(x)
    by_channel = lambda w: np.asarray(w).T.reshape(CT, P, -1)
    three = lambda w: np.concatenate([by_channel(w)] * 3, axis=-1)
    wqk = np.stack([np.stack([three(q), three(k)], axis=2)
                    for q, k in ((L0_conv_q_weight, L0_conv_k_weight), (L1_conv_wf, L1_conv_wg))])
    row = lambda v: np.broadcast_to(np.asarray(v), (P, np.asarray(v).size))
    arrays = {
        "x": x.reshape(BATCH, C, N),
        "wqk": wqk.transpose(2, 0, 1, 3, 4),
        "wv": by_channel(L0_conv_v_weight).transpose(1, 0, 2),
        "wh": by_channel(L1_conv_wh).transpose(1, 0, 2),
        "wo": np.asarray(L1_conv_wv).T,
        "gamma": np.concatenate([row(L0_conv_gamma), row(L1_conv_gamma)], axis=1),
        "b_fg": np.stack([np.concatenate([np.asarray(v)] * 3) for v in (L1_conv_bf, L1_conv_bg)], axis=1),
        "b_h": row(L1_conv_bh),
        "b_o": np.asarray(L1_conv_bv).reshape(CT, P).T,
    }
    arrays = {f"in_{n}": np.ascontiguousarray(a) for n, a in arrays.items()}
    nc = bacc.Bacc("TRN2", target_bir_lowering=False, num_devices=1)
    args = [nc.dram_tensor(n, a.shape, mybir.dt.from_np(a.dtype), kind="ExternalInput").ap()
            for n, a in arrays.items()]
    out = nc.dram_tensor("out", (BATCH, C, N), F32, kind="ExternalOutput").ap()
    build(nc, *args, out)
    r = run_bass_kernel_spmd(nc, [arrays], core_ids=[0])
    return r.results[0]["out"].reshape(x.shape)
```

```python
from contextlib import ExitStack

import concourse.bass as bass
from concourse import mybir

F32 = mybir.dt.float32
F32R = mybir.dt.float32r
ALU = mybir.AluOpType
ACT = mybir.ActivationFunctionType
AX = mybir.AxisListType

P = 128
BATCH, C, N, D = 4, 256, 64 * 64, 32
CT = C // P
KT = N // P
QB = 512
NBLK = N // QB
SUB = QB // P
CHUNK = QB
NCH = N // CHUNK
STACK = 3 * D
MAXROW = STACK
KROWS = STACK + 2
HW = 2 * D + 1
L0_POOL = (0, 5, 8, 11, 13, 14, 15, 21, 27, 29, 31)
L1_POOL = (1, 2, 5, 6, 8, 9, 11, 12, 15, 16, 17, 19, 20, 22, 24, 26, 27, 30)
L1_FULL = (7, 14, 21, 25)
L0_HI_DVE = (1, 5, 9, 11, 13, 14, 17, 19, 21, 23, 25, 27, 29, 31)
L1_HI_DVE = (0, 1, 2, 14, 21, 28, 29, 30, 31)
RING = 8
E_RING = 8
FULL_RING = 4
PRIMED = RING
AHEAD = [4, 4]
SPLIT_AHEAD = [3, 3]
MXSTEPS = [24, 24]
LATE = [2, 4]
EP = [1, 4, 4, 7, 7, 11, 10, 14, 13]
NMX = [3, 4]

HI = [["dve" if j in L0_HI_DVE else "act" for j in range(KT)],
      ["full" if j in L1_FULL else "dve" if j in L1_HI_DVE else "act" for j in range(KT)]]
LO = [["pool" if j in L0_POOL else "dve" for j in range(KT)],
      ["full" if j in L1_FULL else "pool" if j in L1_POOL else "dve" for j in range(KT)]]


COPY_HI = ["dve", "act"]
QK_AT = [1, 2]
HI_STEPS = [2, 4]
LO_STEPS = [4, 2]

PV_ORDER = {0: ((0, 0),), 1: ((1, 0), (0, 1), (1, 1)),
            KT - 2: ((KT - 2, 0),), KT - 1: ((KT - 1, 0), (KT - 2, 1), (KT - 1, 1))}


def count(kinds, kind, g, j):
    return g * kinds.count(kind) + sum(kinds[t % KT] == kind for t in range(j + 1))


def row_tiles(step, layer):
    return [u for u in range(SUB * NCH) if u * MXSTEPS[layer] // (SUB * NCH) == step]


def last_row_step(s, layer):
    return (NCH * s + NCH - 1) * MXSTEPS[layer] // (SUB * NCH)


def build(nc, x, wqk, wv, wh, wo, gamma, b_fg, b_h, b_o, out):
    nc.disable_value_cache = True
    with ExitStack() as ctx:
        def sb(name, shape, dt=F32):
            return ctx.enter_context(nc.sbuf_tensor(name, shape, dt))

        def bank(name):
            return ctx.enter_context(nc.psum_tensor(name, [P, QB], F32))

        def sem(name):
            return ctx.enter_context(nc.semaphore(name))

        def sems(name):
            return [sem(f"{name}{layer}") for layer in range(2)]

        x_sb = sb("x_sb", [P, CT, N])
        qs = sb("q_stack", [P, N], F32R)
        ks = sb("k_stack", [P, N], F32R)
        q_now = sb("q_now", [STACK, SUB, P], F32R)
        e_t = sb("e_t", [P, E_RING, QB])
        p_hi = sb("p_hi", [P, RING, QB], F32R)
        p_lo = sb("p_lo", [P, RING, QB], F32R)
        r_all = sb("r_all", [P, QB])
        o_t = sb("o_t", [P, CT, QB])
        xs = sb("xs", [HW, QB])
        xt = sb("xt", [P, SUB, HW])
        xn = sb("xn", [P, SUB, D])
        x0n = sb("x0n", [D, QB])
        negmax = sb("negmax", [P, SUB, NCH])
        lpart = sb("lpart", [P, SUB, NCH])
        wgt = sb("wgt", [P, SUB, NCH])
        wl = sb("wl", [P, SUB, NCH])
        nm = sb("nm", [P, SUB])
        nm_cols = sb("nm_cols", [P, SUB, KROWS], F32R)
        lsum = sb("lsum", [P, SUB])
        linv = sb("linv", [P, SUB])
        r_col = sb("r_col", [P, SUB])
        l1inv = sb("l1inv", [P, SUB])
        l1r = sb("l1r", [P, SUB])
        ident = sb("ident", [P, P])
        wqk_sb = sb("wqk_sb", [P, 2, CT, 2 * D])
        wv_sb = sb("wv_sb", [P, CT, C])
        wh_sb = sb("wh_sb", [P, CT, D])
        wo_sb = sb("wo_sb", [D, C])
        gam = sb("gam", [P, 2])
        bqk = sb("bqk", [2 * D, 2])
        bh_sb = sb("bh_sb", [P, D])
        bo_sb = sb("bo_sb", [P, CT])
        gbo = sb("gbo", [P, CT])

        with ExitStack() as values:
            v_hi = values.enter_context(nc.sbuf_tensor("v_hi", [P, KT, C], F32R))
            v_lo = values.enter_context(nc.sbuf_tensor("v_lo", [P, KT, C], F32R))
        with ExitStack() as of_layer1:
            def sb1(name, shape, dt=F32):
                return of_layer1.enter_context(nc.sbuf_tensor(name, shape, dt))

            h_f = sb1("h_f", [P, KT, D])
            h_st = sb1("h_st", [P, KT, HW], F32R)
            h_full = sb1("h_full", [P, len(L1_FULL), HW])
            e_full = sb1("e_full", [P, FULL_RING, QB])

        st = [bank("st0"), bank("st1")]
        mx = [bank(f"mx{i}") for i in range(3)]
        acc = [bank("acc0"), bank("acc1")]
        aux = bank("aux")
        row_banks = [mx, [*mx, acc[1]]]
        first_banks = [[aux, mx[2], mx[0], mx[1]], [*mx, aux]]

        w_in, zeroed, ident_ok, gbo_ok = sem("w_in"), sem("zeroed"), sem("ident_ok"), sem("gbo_ok")
        x_in, out_done = [sem(f"x_in{n}") for n in range(NBLK)], sem("out_done")
        qk_psum, qk_hi, qk_lo = sems("qk_psum"), sems("qk_hi"), sems("qk_lo")
        v_psum, v_hi_ok, v_ok = sems("v_psum"), sems("v_hi_ok"), sems("v_ok")
        hf_ok, full_ok = sem("hf_ok"), sem("full_ok")
        q_now_ok = sems("q_now_ok")
        rows_psum, rowmax_ok, rowsum_ok = sems("rows_psum"), sems("rowmax_ok"), sem("rowsum_ok")
        nm_step, nm_rowpsum, nm_rows = sems("nm_step"), sems("nm_rowpsum"), sems("nm_rows")
        wgt_ok, l_step = sem("wgt_ok"), sem("l_step")
        st_psum, exp_ok = sems("st_psum"), sems("exp_ok")
        hi_ok = [{e: sem(f"hi_{e}{n}") for e in ("act", "dve")} for n in range(2)]
        lo_ok = [{e: sem(f"lo_{e}{n}") for e in ("dve", "pool")} for n in range(2)]
        pv_done, acc0_done = sems("pv_done"), sem("acc0_done")
        r_psum, r_ok = sem("r_psum"), sem("r_ok")
        evac, y_ok = [sem("evac_c0"), sem("evac_c1")], sem("y_ok")
        xs_ok, xt_psum, xt_ok, ep_step = sem("xs_ok"), sem("xt_psum"), sem("xt_ok"), sem("ep_step")
        x0_psum, x0_ok, o_psum, o_ok = sem("x0_psum"), sem("x0_ok"), sem("o_psum"), sem("o_ok")

        block = ctx.enter_context(nc.Block())
        ZEROED = 3


        def cols(ib, at=0, n=QB):
            return bass.ds(ib * QB + at, n)

        def e_read(eng, g, j, layer):
            kind = LO[layer][j % KT]
            if kind != "full":
                eng.wait_ge(lo_ok[layer][kind], count(LO[layer], kind, g, j))

        def take_lo(eng, kind, g, j, layer, free):
            if LO[layer][j % KT] != kind:
                return
            by = HI[layer][j % KT]
            eng.wait_ge(hi_ok[layer][by], count(HI[layer], by, g, j))
            if free:
                eng.wait_ge(pv_done[layer], PRIMED + g * KT + j + 1 - RING)
            eng.tensor_tensor(p_lo[:, j % RING, :], e_t[:, j % E_RING, :], p_hi[:, j % RING, :].bitcast(F32),
                              ALU.subtract).then_inc(lo_ok[layer][kind], 1)

        def blocks(eng, body, first_differs):
            if first_differs:
                body(0, True, False)
            with_first = 1 if first_differs else 0
            with eng.Fori(with_first, NBLK - 1) as ib:
                body(ib, False, False)
            body(NBLK - 1, False, True)

        @block.sync
        def _(eng):
            eng.sem_inc(out_done, PRIMED)

            def load(b, n):
                at = slice(n * QB, (n + 1) * QB)
                eng.dma_start(x_sb[:, :, at], x[b].rearrange("(k p) n -> p k n", p=P)[:, :, at])\
                   .then_inc(x_in[n], 16)

            def store(b, ib):
                eng.wait_ge(o_ok, PRIMED + (b * NBLK + ib) * 2 + 2)
                eng.dma_start(out[b].rearrange("(k p) n -> p k n", p=P)[:, :, cols(ib)],
                              o_t[:, :, :]).then_inc(out_done, 16)

            for sbuf, dram in ((wqk_sb[:, :, :, :], wqk), (wv_sb[:, :, :], wv), (wh_sb[:, :, :], wh),
                               (wo_sb[:, :], wo), (gam[:, :], gamma), (bh_sb[:, :], b_h),
                               (bo_sb[:, :], b_o), (bqk[:, 1:2], b_fg)):
                eng.dma_start(sbuf, dram).then_inc(w_in, 16)
            for n in range(NBLK):
                load(0, n)
            for b in range(BATCH):
                for n in range(NBLK):
                    store(b, n)
                    if b < BATCH - 1:
                        load(b + 1, n)
            eng.wait_ge(out_done, PRIMED + 16 * BATCH * NBLK)

        @block.gpsimd
        def _(eng):
            eng.sem_inc(y_ok, PRIMED)
            eng.memset(ident[:, :], 0.0).then_inc(ident_ok, 1)
            eng.wait_ge(ident_ok, 1)
            eng.affine_select(out=ident[:, :], in_=ident[:, :], compare_op=ALU.not_equal, fill=1.0,
                              base=0, pattern=[[-1, P]], channel_multiplier=1).then_inc(ident_ok, 1)

            def fill(g, blk, s, layer):
                eng.wait_ge(rows_psum[layer], (g - 1) * SUB * NCH + NCH * (s + 1))
                eng.tensor_copy(q_now[:, s, :], qs[0:STACK, cols(blk, s * P, P)])\
                   .then_inc(q_now_ok[layer], 1)

            def residual(g, ib):
                for c in range(CT):
                    eng.wait_ge(evac[c], PRIMED + g + 1)
                    ins = eng.tensor_tensor(x_sb[:, c, cols(ib)], x_sb[:, c, cols(ib)], o_t[:, c, :], ALU.add)
                ins.then_inc(y_ok, 1)

            with eng.Fori(0, BATCH) as b:
                for layer in range(2):
                    g0 = b * NBLK
                    for j in range(SPLIT_AHEAD[layer]):
                        take_lo(eng, "pool", g0, j, layer, False)

                    def body(ib, fills, last):
                        g = g0 + ib
                        for j in range(KT):
                            if not last or j + SPLIT_AHEAD[layer] < KT:
                                take_lo(eng, "pool", g, j + SPLIT_AHEAD[layer], layer, True)
                            for s in range(SUB):
                                if fills and j == last_row_step(s, layer) + 1:
                                    fill(g + 2, ib + 2, s, layer)
                        if layer == 0:
                            residual(g, ib)

                    with eng.Fori(0, NBLK - 2) as ib:
                        body(ib, True, False)
                    body(NBLK - 2, False, False)
                    body(NBLK - 1, False, True)

        @block.tensor
        def _(eng):
            def project_qk(b, g0, n, layer):
                if layer == 0:
                    eng.wait_ge(x_in[n], 16 * (b + 1))
                else:
                    eng.wait_ge(y_ok, PRIMED + g0 + n + 1)
                if n > 1:
                    eng.wait_ge(qk_lo[layer], LO_STEPS[layer] * (g0 + n - 1))
                for k in range(CT):
                    mm = eng.matmul(st[n % 2][0:2 * D, :], wqk_sb[:, layer, k, :],
                                    x_sb[:, k, n * QB:(n + 1) * QB], start=(k == 0), stop=(k == 1))
                mm.then_inc(qk_psum[layer], 1)

            def project_v(g0, t):
                pair, i = divmod(t, 2)
                if pair >= 2 and i == 0:
                    eng.wait_ge(v_ok[0], 2 * g0 + pair - 1)
                for k in range(CT):
                    mm = eng.matmul(acc[pair % 2][:, i * C:(i + 1) * C], x_sb[:, k, t * P:(t + 1) * P],
                                    wv_sb[:, k, :], start=(i == 0 and k == 0), stop=(i == 1 and k == 1),
                                    skip_group_check=True)
                if i == 1:
                    mm.then_inc(v_psum[0], 1)

            def project_h(t):
                half, i = divmod(t, KT // 2)
                for k in range(CT):
                    mm = eng.matmul(acc[half][:, i * D:(i + 1) * D], x_sb[:, k, t * P:(t + 1) * P],
                                    wh_sb[:, k, :], start=(i == 0 and k == 0), stop=(i == KT // 2 - 1 and k == 1),
                                    skip_group_check=True)
                if i == KT // 2 - 1:
                    mm.then_inc(v_psum[1], 1)

            def row_tile(g, u, s, c, layer, to, wait_for):
                if wait_for is not None:
                    used = rowsum_ok if layer == 0 else rowmax_ok[1]
                    eng.wait_ge(used, g * SUB * NCH + wait_for + 1)
                eng.matmul(to[:, :], q_now[:, s, :], ks[0:STACK, c * CHUNK:(c + 1) * CHUNK],
                           start=True, stop=True).then_inc(rows_psum[layer], 1)

            def rows(g, u, layer):
                turns = NMX[layer]
                before = u - turns if u >= turns else max(v for v in range(SUB * NCH) if v % turns == u) - SUB * NCH
                row_tile(g, u, u // NCH, u % NCH, layer, row_banks[layer][u % turns], before)

            def first_row(g, c, s, layer):
                if s == 0:
                    eng.wait_ge(qk_lo[layer], LO_STEPS[layer] * (g + c + 1))
                    if c == 0:
                        eng.wait_ge(q_now_ok[layer], g * SUB + SUB)
                u, turns = SUB * c + s, SUB
                row_tile(g, u, s, c, layer, first_banks[layer][u % turns], u - turns if u >= turns else None)

            def max_rows(g, s, layer, groups):
                eng.wait_ge(nm_step[layer], 3 * (g * SUB + groups))
                return eng.transpose(aux[0:KROWS, s * P:(s + 1) * P], nm_cols[:, s, :].bitcast(F32), ident[:, :])

            def factor_rows(g):
                eng.wait_ge(l_step, 4 * (g * SUB + SUB))
                for s in range(SUB):
                    mm = eng.transpose(aux[:, s * P:(s + 1) * P], r_col[:, s:s + 1].to_broadcast([P, P]),
                                       ident[:, :])
                mm.then_inc(r_psum, 1)

            def scores_t(g, ib, j, layer, free):
                if j % KT == 0:
                    eng.wait_ge(nm_rows[layer], (g + j // KT) * SUB + SUB)
                if free:
                    eng.wait_ge(exp_ok[layer], g * KT + j - 1)
                eng.matmul(st[j % 2][:, :], ks[0:KROWS, (j % KT) * P:(j % KT + 1) * P],
                           qs[0:KROWS, cols(ib + j // KT)], start=True, stop=True).then_inc(st_psum[layer], 1)

            def sums0(g, j):
                eng.wait_ge(lo_ok[0][LO[0][j]], count(LO[0], LO[0][j], g, j))
                for t, c in PV_ORDER.get(j, ((j, 0), (j, 1))):
                    a, b = p_hi[:, t % RING, :], p_lo[:, t % RING, :]
                    hi, lo = v_hi[:, t, c * P:(c + 1) * P], v_lo[:, t, c * P:(c + 1) * P]
                    if t == 0:
                        eng.wait_ge(evac[c], PRIMED + g)
                    eng.matmul(acc[c][:, :], hi, a, start=(t == 0), stop=False)
                    eng.matmul(acc[c][:, :], lo, a, start=False, stop=False)
                    mm = eng.matmul(acc[c][:, :], hi, b, start=False, stop=(t == KT - 1))
                    if c == 1:
                        mm.then_inc(pv_done[0], 1)
                    elif t == KT - 1:
                        mm.then_inc(acc0_done, 1)

            def sums1(g, j):
                kind = LO[1][j]
                if kind == "full":
                    eng.wait_ge(exp_ok[1], g * KT + j + 1)
                else:
                    eng.wait_ge(lo_ok[1][kind], count(LO[1], kind, g, j))
                if j == 0:
                    eng.wait_ge(xs_ok, PRIMED + g)
                if kind == "full":
                    terms = [(h_full[:, L1_FULL.index(j), :], e_full[:, L1_FULL.index(j) % FULL_RING, :])]
                else:
                    terms = [(h_st[:, j, :], p[:, j % RING, :]) for p in (p_hi, p_lo)]
                for n, (h, p) in enumerate(terms):
                    mm = eng.matmul(acc[0][0:HW, :], h, p, start=(j == 0 and n == 0),
                                    stop=(j == KT - 1 and n == len(terms) - 1))
                mm.then_inc(pv_done[1], 1)

            def turn_sums(g):
                eng.wait_ge(xs_ok, PRIMED + g + 1)
                for s in range(SUB):
                    mm = eng.transpose(aux[:, s * HW:(s + 1) * HW], xs[:, s * P:(s + 1) * P], ident[0:HW, 0:HW])
                mm.then_inc(xt_psum, 1)

            def turn_back(g):
                eng.wait_ge(ep_step, 4 * g + 4)
                for s in range(SUB):
                    mm = eng.transpose(aux[0:D, s * P:(s + 1) * P], xn[:, s, :], ident[:, :])
                mm.then_inc(x0_psum, 1)

            def widen(g, c, to):
                if c == 0:
                    eng.wait_ge(x0_ok, g + 1)
                eng.matmul(to[:, :], wo_sb[:, c * P:(c + 1) * P], x0n[:, :], start=True, stop=True)\
                   .then_inc(o_psum, 1)

            for done in pv_done:
                eng.sem_inc(done, PRIMED)
            eng.wait_ge(w_in, 16 * 8)
            eng.wait_ge(ident_ok, 2)
            eng.wait_ge(zeroed, ZEROED)
            with eng.Fori(0, BATCH) as b:
                for layer in range(2):
                    g0 = b * NBLK
                    project_qk(b, g0, 0, layer)
                    for n in range(NBLK):
                        for s in range(SUB):
                            t = SUB * n + s
                            if layer == 0:
                                if t == 2:
                                    eng.wait_ge(o_ok, PRIMED + 2 * g0)
                                project_v(g0, t)
                            else:
                                if t % (KT // 2) == 0:
                                    eng.wait_ge(evac[2 * t // KT], PRIMED + g0 + NBLK)
                                project_h(t)
                            if n:
                                first_row(g0, n - 1, s, layer)
                            if s == QK_AT[layer] and n < NBLK - 1:
                                project_qk(b, g0, n + 1, layer)
                    for s in range(SUB):
                        first_row(g0, NBLK - 1, s, layer)
                    if layer == 0:
                        eng.wait_ge(rowsum_ok, (g0 + 1) * SUB * NCH - 3)
                    for s in range(SUB):
                        mm = max_rows(g0, s, layer, SUB)
                    mm.then_inc(nm_rowpsum[layer], SUB)
                    for j in range(AHEAD[layer]):
                        if j == AHEAD[layer] - 1:
                            eng.wait_ge(v_ok[layer], 2 * g0 + 2 * NBLK if layer == 0 else 2 * b + 2)
                            if layer == 1:
                                eng.wait_ge(full_ok, (len(L1_FULL) + 3) * (b + 1))
                        scores_t(g0, 0, j, layer, j >= 2)

                    def body(ib, first, last):
                        g = g0 + ib
                        for j in range(KT):
                            if not last or j + AHEAD[layer] < KT:
                                scores_t(g, ib, j + AHEAD[layer], layer, True)
                            if not last:
                                for u in row_tiles(j, layer):
                                    if u % NCH == 0:
                                        eng.wait_ge(q_now_ok[layer], (g + 1) * SUB + u // NCH + 1)
                                    rows(g + 1, u, layer)
                                for s in range(SUB):
                                    if j == last_row_step(s, layer) + LATE[layer]:
                                        if s:
                                            eng.wait_ge(nm_rows[layer], (g + 1) * SUB + s)
                                        elif layer == 0:
                                            eng.wait_ge(r_ok, PRIMED + g + 1)
                                        elif not first:
                                            eng.wait_ge(x0_ok, g)
                                        if layer == 1 and s == 1 and not first:
                                            eng.wait_ge(o_ok, PRIMED + 2 * g)
                                        max_rows(g + 1, s, layer, s + 1).then_inc(nm_rowpsum[layer], 1)
                            if layer == 0:
                                if j == 2:
                                    factor_rows(g)
                                sums0(g, j)
                            else:
                                if not first and j == EP[0]:
                                    turn_sums(g - 1)
                                if not first and j == EP[3]:
                                    turn_back(g - 1)
                                if not first and j == EP[5]:
                                    if not last:
                                        eng.wait_ge(nm_rows[1], (g + 1) * SUB + 1)
                                    widen(g - 1, 0, aux)
                                if not first and j == EP[7]:
                                    eng.wait_ge(o_ok, PRIMED + 2 * g - 1)
                                    widen(g - 1, 1, aux)
                                sums1(g, j)

                    blocks(eng, body, layer == 1)
                    if layer == 1:
                        turn_sums(g0 + NBLK - 1)
                        turn_back(g0 + NBLK - 1)
                        for c, to in enumerate((acc[1], aux)):
                            widen(g0 + NBLK - 1, c, to)

        @block.scalar
        def _(eng):
            def stack_hi(g0, n, layer):
                for r, (to, places) in enumerate(((qs, (0, 2)), (ks, (0, 1)))):
                    for i, at in enumerate(places if COPY_HI[layer] == "act" else places[:1]):
                        if i == 0 and r == 0:
                            eng.wait_ge(qk_psum[layer], g0 + n + 1)
                        eng.activation(to[at * D:(at + 1) * D, n * QB:(n + 1) * QB],
                                       st[n % 2][r * D:(r + 1) * D, :], ACT.Identity,
                                       bias=bqk[r * D:(r + 1) * D, layer:layer + 1]).then_inc(qk_hi[layer], 1)

            def first_queries(g, blk, layer):
                if blk == 0:
                    eng.wait_ge(qk_lo[layer], LO_STEPS[layer] * g + LO_STEPS[layer] // 2)
                else:
                    eng.wait_ge(rows_psum[layer], (g + 1) * SUB * NCH)
                eng.activation(q_now[:, :, :], qs[0:STACK, blk * QB:(blk + 1) * QB].bitcast(F32), ACT.Copy)\
                   .then_inc(q_now_ok[layer], SUB)

            def rowsum(g, u, s, c, of):
                eng.wait_ge(rowmax_ok[0], g * SUB * NCH + u + 1)
                eng.activation(of[u % len(of)][:, :], of[u % len(of)][:, :], ACT.Exp, bias=negmax[:, s, c:c + 1],
                               accum_out=lpart[:, s, c:c + 1]).then_inc(rowsum_ok, 1)

            def weights(g, s, first):
                eng.wait_ge(nm_step[0], 3 * g * SUB + (SUB if first else 3 * s + 1))
                eng.activation(wgt[:, s, :], negmax[:, s, :], ACT.Exp, scale=-1.0,
                               bias=nm[:, s:s + 1]).then_inc(wgt_ok, 1)

            def put_max_rows(g, blk, s, n, layer):
                eng.wait_ge(nm_rowpsum[layer], g * SUB + s + n)
                eng.activation(qs[MAXROW:KROWS, cols(blk, s * P, n * P)], aux[MAXROW:KROWS, s * P:(s + n) * P],
                               ACT.Copy).then_inc(nm_rows[layer], n)

            def exps(g, j, layer, free):
                eng.wait_ge(st_psum[layer], g * KT + j + 1)
                to = e_t[:, j % E_RING, :]
                if LO[layer][j % KT] == "full":
                    i = L1_FULL.index(j)
                    if i >= FULL_RING:
                        eng.wait_ge(pv_done[1], PRIMED + g * KT + L1_FULL[i - FULL_RING] + 1)
                    to = e_full[:, i % FULL_RING, :]
                elif free:
                    e_read(eng, g, j - E_RING, layer)
                eng.activation(to, st[j % 2][:, :], ACT.Exp).then_inc(exp_ok[layer], 1)

            def hi(g, j, layer, free):
                if HI[layer][j % KT] != "act":
                    return
                eng.wait_ge(exp_ok[layer], g * KT + j + 1)
                if free:
                    eng.wait_ge(pv_done[layer], PRIMED + g * KT + j + 1 - RING)
                eng.activation(p_hi[:, j % RING, :], e_t[:, j % E_RING, :], ACT.Copy)\
                   .then_inc(hi_ok[layer]["act"], 1)

            def put_factors(g):
                eng.wait_ge(r_psum, g + 1)
                eng.wait_ge(evac[1], PRIMED + g)
                eng.activation(r_all[:, :], aux[:, :], ACT.Copy).then_inc(r_ok, 1)

            for done in (r_ok, xs_ok):
                eng.sem_inc(done, PRIMED)
            def h_hi(b, half):
                t = slice(half * KT // 2, (half + 1) * KT // 2)
                eng.wait_ge(hf_ok, 2 * b + half + 1)
                eng.activation(h_st[:, t, 0:D], h_f[:, t, :], ACT.Copy).then_inc(v_hi_ok[1], 1)

            eng.wait_ge(w_in, 16 * 8)
            eng.wait_ge(zeroed, ZEROED)
            with eng.Fori(0, BATCH) as b:
                for layer in range(2):
                    g0 = b * NBLK
                    stack_hi(g0, 0, layer)
                    first_queries(g0, 0, layer)
                    for n in range(NBLK):
                        for s in range(SUB):
                            if layer == 0 and s % 2 == 1:
                                pair = 2 * n + s // 2
                                eng.wait_ge(v_psum[0], 2 * g0 + pair + 1)
                                eng.activation(v_hi[:, 2 * pair:2 * pair + 2, :], acc[pair % 2][:, :], ACT.Copy)\
                                   .then_inc(v_hi_ok[0], 1)
                            u = SUB * (n - 1) + s - 1
                            if layer == 0 and u >= 0:
                                rowsum(g0, u, u % SUB, u // SUB, first_banks[0])
                            if s == 2 and n < NBLK - 1:
                                stack_hi(g0, n + 1, layer)
                        if layer == 1 and n == NBLK - 1:
                            h_hi(b, 0)
                    if layer == 0:
                        for u in range(SUB * (NBLK - 1) - 1, SUB * NBLK):
                            rowsum(g0, u, u % SUB, u // SUB, first_banks[0])
                    put_max_rows(g0, 0, 0, SUB, layer)
                    for j in range(AHEAD[layer]):
                        exps(g0, j, layer, j >= E_RING)
                        if j == 1:
                            first_queries(g0, 1, layer)
                            if layer == 0:
                                for s in range(SUB):
                                    weights(g0, s, True)
                            else:
                                h_hi(b, 1)
                        if j >= AHEAD[layer] - SPLIT_AHEAD[layer]:
                            hi(g0, j - AHEAD[layer] + SPLIT_AHEAD[layer], layer, False)

                    def body(ib, first, last):
                        g = g0 + ib
                        for j in range(KT):
                            if not last or j + AHEAD[layer] < KT:
                                exps(g, j + AHEAD[layer], layer, True)
                            if not last or j + SPLIT_AHEAD[layer] < KT:
                                hi(g, j + SPLIT_AHEAD[layer], layer, True)
                            if not last:
                                if layer == 0:
                                    for u in row_tiles(j, layer):
                                        rowsum(g + 1, u, u // NCH, u % NCH, row_banks[0])
                                        if u % NCH == NCH - 1:
                                            weights(g + 1, u // NCH, False)
                                for s in range(SUB):
                                    if j == last_row_step(s, layer) + LATE[layer]:
                                        put_max_rows(g + 1, ib + 1, s, 1, layer)
                            if layer == 0 and j == 3:
                                put_factors(g)
                            if layer == 1 and not first and j == EP[1]:
                                take_turned(g - 1)
                            if layer == 1 and not first and j == EP[4]:
                                take_back(g - 1)
                        if layer == 1:
                            eng.wait_ge(pv_done[1], PRIMED + g * KT + KT)
                            eng.activation(xs[:, :], acc[0][0:HW, :], ACT.Copy).then_inc(xs_ok, 1)

                    def take_turned(g):
                        eng.wait_ge(xt_psum, g + 1)
                        eng.activation(xt[:, :, :], aux[:, 0:SUB * HW], ACT.Copy).then_inc(xt_ok, 1)

                    def take_back(g):
                        eng.wait_ge(x0_psum, g + 1)
                        eng.activation(x0n[:, :], aux[0:D, :], ACT.Copy).then_inc(x0_ok, 1)

                    blocks(eng, body, layer == 1)
                    if layer == 1:
                        take_turned(g0 + NBLK - 1)
                        take_back(g0 + NBLK - 1)

        @block.vector
        def _(eng):
            def stack_lo(g0, n, r, layer):
                to, lo, copy = ((qs, 1, 2), (ks, 2, 1))[r]
                cut, steps, here = slice(n * QB, (n + 1) * QB), HI_STEPS[layer], slice(r * D, (r + 1) * D)
                eng.wait_ge(qk_hi[layer], steps * (g0 + n) + steps // 2 * (r + 1))
                eng.scalar_tensor_tensor(to[lo * D:(lo + 1) * D, cut], st[n % 2][here, :],
                                         bqk[here, layer:layer + 1], to[0:D, cut].bitcast(F32),
                                         ALU.add, ALU.subtract).then_inc(qk_lo[layer], 1)
                if COPY_HI[layer] == "dve":
                    eng.tensor_copy(to[copy * D:(copy + 1) * D, cut], to[0:D, cut].bitcast(F32))\
                       .then_inc(qk_lo[layer], 1)

            def rowmax(g, u, s, c, layer, of):
                eng.wait_ge(rows_psum[layer], g * SUB * NCH + u + 1)
                eng.tensor_reduce(negmax[:, s, c:c + 1], of[u % len(of)][:, :], AX.X, ALU.max, negate=True)\
                   .then_inc(rowmax_ok[layer], 1)

            def maximum(g, s, n, parts, layer):
                to, done = slice(s, s + n), 3 * (g * SUB + s)
                eng.wait_ge(rowmax_ok[layer], g * SUB * NCH + parts)
                eng.tensor_reduce(nm[:, to], negmax[:, to, :], AX.X, ALU.min).then_inc(nm_step[layer], n)
                eng.wait_ge(nm_step[layer], done + n)
                whole = nm[:, to].rearrange("p (s a) -> p s a", a=1)
                hi, lo = nm_cols[:, to, MAXROW:MAXROW + 1], nm_cols[:, to, MAXROW + 1:KROWS]
                eng.tensor_copy(hi, whole).then_inc(nm_step[layer], n)
                eng.wait_ge(nm_step[layer], done + 2 * n)
                eng.tensor_tensor(lo, whole, hi.bitcast(F32), ALU.subtract).then_inc(nm_step[layer], n)

            def factor(g, s, n, free):
                to, done = slice(s, s + n), 4 * (g * SUB + s)
                eng.wait_ge(wgt_ok, g * SUB + s + n)
                eng.tensor_tensor(wl[:, to, :], wgt[:, to, :], lpart[:, to, :], ALU.mult).then_inc(l_step, n)
                eng.wait_ge(l_step, done + n)
                eng.tensor_reduce(lsum[:, to], wl[:, to, :], AX.X, ALU.add).then_inc(l_step, n)
                eng.wait_ge(l_step, done + 2 * n)
                eng.reciprocal(linv[:, to], lsum[:, to]).then_inc(l_step, n)
                eng.wait_ge(l_step, done + 3 * n)
                if free:
                    eng.wait_ge(r_psum, g)
                eng.tensor_scalar(r_col[:, to], linv[:, to], gam[:, 0:1], None, ALU.mult)\
                   .then_inc(l_step, n)

            def split(g, j, layer, free):
                if HI[layer][j % KT] == "dve":
                    eng.wait_ge(exp_ok[layer], g * KT + j + 1)
                    if free:
                        eng.wait_ge(pv_done[layer], PRIMED + g * KT + j + 1 - RING)
                    eng.tensor_copy(p_hi[:, j % RING, :], e_t[:, j % E_RING, :]).then_inc(hi_ok[layer]["dve"], 1)
                take_lo(eng, "dve", g, j, layer, free)

            def take_sums(g):
                eng.wait_ge(r_ok, PRIMED + g + 1)
                for c in range(CT):
                    if c == 0:
                        eng.wait_ge(acc0_done, g + 1)
                        eng.wait_ge(y_ok, PRIMED + g)
                    else:
                        eng.wait_ge(pv_done[0], PRIMED + g * KT + KT)
                    eng.tensor_tensor(o_t[:, c, :], acc[c][:, :], r_all[:, :], ALU.mult).then_inc(evac[c], 1)

            def normalise(g):
                eng.wait_ge(xt_ok, g + 1)
                eng.reciprocal(l1inv[:, :], xt[:, :, 2 * D:HW]).then_inc(ep_step, 1)
                eng.tensor_tensor(xt[:, :, 0:D], xt[:, :, 0:D], xt[:, :, D:2 * D], ALU.add).then_inc(ep_step, 1)
                eng.wait_ge(ep_step, 4 * g + 2)
                eng.tensor_scalar(l1r[:, :], l1inv[:, :], gam[:, 1:2], None, ALU.mult).then_inc(ep_step, 1)
                eng.wait_ge(ep_step, 4 * g + 3)
                eng.tensor_tensor(xn[:, :, :], xt[:, :, 0:D],
                                  l1r[:, :].rearrange("p (s a) -> p s a", a=1).to_broadcast([P, SUB, D]),
                                  ALU.mult).then_inc(ep_step, 1)

            def finish(g, ib, c, at):
                if c == 0:
                    eng.wait_ge(out_done, PRIMED + 16 * g)
                eng.wait_ge(o_psum, 2 * g + c + 1)
                eng.scalar_tensor_tensor(o_t[:, c, :], at[:, :], gbo[:, c:c + 1], x_sb[:, c, cols(ib)],
                                         ALU.add, ALU.add).then_inc(o_ok, 1)

            for done in (*evac, o_ok):
                eng.sem_inc(done, PRIMED)
            eng.memset(bqk[:, 0:1], 0.0).then_inc(zeroed, 1)
            eng.memset(ks[MAXROW:KROWS, :].bitcast(F32), 1.0).then_inc(zeroed, 1)
            eng.memset(nm_cols[:, :, :].bitcast(F32), 0.0).then_inc(zeroed, 1)
            eng.wait_ge(w_in, 16 * 8)
            eng.wait_ge(zeroed, ZEROED)
            def h_ones():
                eng.memset(h_st[:, :, 2 * D:HW].bitcast(F32), 1.0).then_inc(full_ok, 1)
                eng.memset(h_full[:, :, D:2 * D], 0.0).then_inc(full_ok, 1)
                eng.memset(h_full[:, :, 2 * D:HW], 1.0).then_inc(full_ok, 1)

            def h_whole(b, half):
                t = slice(half * KT // 2, (half + 1) * KT // 2)
                eng.wait_ge(v_psum[1], 2 * b + half + 1)
                eng.tensor_tensor(h_f[:, t, :], acc[half][:, :].rearrange("p (t d) -> p t d", d=D),
                                  bh_sb[:, :].rearrange("p (a d) -> p a d", a=1).to_broadcast([P, KT // 2, D]),
                                  ALU.add).then_inc(hf_ok, 1)

            def h_lo(b, half):
                t = slice(half * KT // 2, (half + 1) * KT // 2)
                eng.wait_ge(v_hi_ok[1], 2 * b + half + 1)
                eng.tensor_tensor(h_st[:, t, D:2 * D], h_f[:, t, :], h_st[:, t, 0:D].bitcast(F32),
                                  ALU.subtract).then_inc(v_ok[1], 1)
                for i, tile in enumerate(L1_FULL):
                    if tile // (KT // 2) == half:
                        eng.tensor_copy(h_full[:, i, 0:D], h_f[:, tile, :]).then_inc(full_ok, 1)

            def values_lo(g0, pair):
                t = slice(2 * pair, 2 * pair + 2)
                eng.wait_ge(v_hi_ok[0], 2 * g0 + pair + 1)
                eng.tensor_tensor(v_lo[:, t, :], acc[pair % 2][:, :].rearrange("p (t c) -> p t c", t=2),
                                  v_hi[:, t, :].bitcast(F32), ALU.subtract).then_inc(v_ok[0], 1)

            eng.tensor_scalar(gbo[:, :], bo_sb[:, :], gam[:, 1:2], None, ALU.mult).then_inc(gbo_ok, 1)
            eng.wait_ge(gbo_ok, 1)
            with eng.Fori(0, BATCH) as b:
                for layer in range(2):
                    g0 = b * NBLK
                    if layer == 1:
                        h_ones()
                    for n in range(NBLK):
                        for s in range(SUB):
                            if layer == 0 and s < 2:
                                stack_lo(g0, n, s, layer)
                            if n:
                                rowmax(g0, SUB * (n - 1) + s, s, n - 1, layer, first_banks[layer])
                            if layer == 1 and s < 2:
                                stack_lo(g0, n, s, layer)
                            if layer == 0 and s % 2 == 0 and 2 * n + s // 2 > 0:
                                values_lo(g0, 2 * n + s // 2 - 1)
                        if layer == 1 and n == NBLK // 2:
                            h_whole(b, 0)
                    for s in range(SUB):
                        rowmax(g0, SUB * (NBLK - 1) + s, s, NBLK - 1, layer, first_banks[layer])
                    maximum(g0, 0, SUB, SUB * NCH, layer)
                    if layer == 0:
                        values_lo(g0, 2 * NBLK - 1)
                        factor(g0, 0, SUB, False)
                    else:
                        h_whole(b, 1)
                        h_lo(b, 0)
                        h_lo(b, 1)
                    for j in range(SPLIT_AHEAD[layer]):
                        split(g0, j, layer, False)

                    def body(ib, first, last):
                        g = g0 + ib
                        for j in range(KT):
                            if not last:
                                for u in row_tiles(j, layer):
                                    s, c = divmod(u, NCH)
                                    rowmax(g + 1, u, s, c, layer, row_banks[layer])
                                    if c == NCH - 1:
                                        maximum(g + 1, s, 1, u + 1, layer)
                                if layer == 0:
                                    for s in range(SUB):
                                        if j == last_row_step(s, layer) + LATE[layer]:
                                            factor(g + 1, s, 1, True)
                            if layer == 0 and j == KT - 1:
                                take_sums(g)
                            if not last or j + SPLIT_AHEAD[layer] < KT:
                                split(g, j + SPLIT_AHEAD[layer], layer, True)
                            if layer == 1 and not first and j == EP[2]:
                                normalise(g - 1)
                            if layer == 1 and not first and j in EP[6::2]:
                                finish(g - 1, ib - 1, EP[6::2].index(j), aux)

                    blocks(eng, body, layer == 1)
                    if layer == 1:
                        normalise(g0 + NBLK - 1)
                        for c, at in enumerate((acc[1], aux)):
                            finish(g0 + NBLK - 1, NBLK - 1, c, at)


def kernel(x, L0_conv_q_weight, L0_conv_k_weight, L0_conv_v_weight, L0_conv_gamma,
           L1_conv_wf, L1_conv_bf, L1_conv_wg, L1_conv_bg, L1_conv_wh, L1_conv_bh,
           L1_conv_wv, L1_conv_bv, L1_conv_gamma):
    import numpy as np
    from concourse import bacc
    from concourse.bass_utils import run_bass_kernel_spmd

    x = np.asarray(x)
    by_channel = lambda w: np.asarray(w).T.reshape(CT, P, -1)
    wqk = np.stack([np.concatenate([by_channel(q), by_channel(k)], axis=2)
                    for q, k in ((L0_conv_q_weight, L0_conv_k_weight), (L1_conv_wf, L1_conv_wg))])
    row = lambda v: np.broadcast_to(np.asarray(v), (P, np.asarray(v).size))
    arrays = {
        "x": x.reshape(BATCH, C, N),
        "wqk": wqk.transpose(2, 0, 1, 3),
        "wv": by_channel(L0_conv_v_weight).transpose(1, 0, 2),
        "wh": by_channel(L1_conv_wh).transpose(1, 0, 2),
        "wo": np.asarray(L1_conv_wv).T,
        "gamma": np.concatenate([row(L0_conv_gamma), row(L1_conv_gamma)], axis=1),
        "b_fg": np.concatenate([np.asarray(L1_conv_bf), np.asarray(L1_conv_bg)])[:, None],
        "b_h": row(L1_conv_bh),
        "b_o": np.asarray(L1_conv_bv).reshape(CT, P).T,
    }
    arrays = {f"in_{n}": np.ascontiguousarray(a) for n, a in arrays.items()}
    nc = bacc.Bacc("TRN2", target_bir_lowering=False, num_devices=1)
    args = [nc.dram_tensor(n, a.shape, mybir.dt.from_np(a.dtype), kind="ExternalInput").ap()
            for n, a in arrays.items()]
    out = nc.dram_tensor("out", (BATCH, C, N), F32, kind="ExternalOutput").ap()
    build(nc, *args, out)
    r = run_bass_kernel_spmd(nc, [arrays], core_ids=[0])
    return r.results[0]["out"].reshape(x.shape)
```

```python
from contextlib import ExitStack

import concourse.bass as bass
from concourse import mybir

F32 = mybir.dt.float32
F32R = mybir.dt.float32r
ALU = mybir.AluOpType
ACT = mybir.ActivationFunctionType
AX = mybir.AxisListType

P = 128
BATCH, C, N, D = 4, 256, 64 * 64, 32
CT = C // P
KT = N // P
QB = 512
NBLK = N // QB
SUB = QB // P
CHUNK = QB
NCH = N // CHUNK
STACK = 3 * D
MAXROW = STACK
KROWS = STACK + 2
HW = 2 * D + 1

L0_POOL = (0, 4, 5, 8, 11, 13, 14, 16, 20, 21, 22, 23, 29, 31)
L0_HI_DVE = (1, 5, 8, 9, 11, 13, 14, 17, 19, 23, 25, 27, 28, 29, 30, 31)
L1_POOL = (1, 2, 5, 6, 8, 10, 11, 12, 15, 16, 17, 18, 19, 22, 23, 24, 26, 28, 30)
L1_HI_DVE = (0, 1, 2, 28, 29, 30, 31)
L1_FULL = (7, 14, 20, 25, 27)
HI = [["dve" if j in L0_HI_DVE else "act" for j in range(KT)],
      ["full" if j in L1_FULL else "dve" if j in L1_HI_DVE else "act" for j in range(KT)]]
LO = [["pool" if j in L0_POOL else "dve" for j in range(KT)],
      ["full" if j in L1_FULL else "pool" if j in L1_POOL else "dve" for j in range(KT)]]

RING = 8
E_RING = 8
FULL_RING = 4
PRIMED = RING
AHEAD = [4, 4]
SPLIT_AHEAD = [3, 3]
MXSTEPS = [24, 24]
LATE = [2, 4]
NMX = [3, 4]

TURN_SUMS, TAKE_TURNED, NORMALISE, TURN_BACK, TAKE_BACK = 1, 4, 4, 7, 7
WIDEN, FINISH = (11, 14), (10, 13)

COPY_HI = ["dve", "act"]
QK_AT = [(1, 2), (1, 2)]
HI_STEPS = [2, 4]
LO_STEPS = [4, 2]

PV_ORDER = {0: ((0, 0),), 1: ((1, 0), (0, 1), (1, 1)),
            KT - 2: ((KT - 2, 0),), KT - 1: ((KT - 1, 0), (KT - 2, 1), (KT - 1, 1))}


def count(kinds, kind, g, j):
    return g * kinds.count(kind) + sum(kinds[t % KT] == kind for t in range(j + 1))


def row_tiles(step, layer):
    return [u for u in range(SUB * NCH) if u * MXSTEPS[layer] // (SUB * NCH) == step]


def last_row_step(s, layer):
    return (NCH * s + NCH - 1) * MXSTEPS[layer] // (SUB * NCH)


def build(nc, x, wqk, wqkh, wv, wo, gamma, b_qkh, b_o, out):
    nc.disable_value_cache = True
    with ExitStack() as ctx:
        def sb(name, shape, dt=F32):
            return ctx.enter_context(nc.sbuf_tensor(name, shape, dt))

        def bank(name):
            return ctx.enter_context(nc.psum_tensor(name, [P, QB], F32))

        def sem(name):
            return ctx.enter_context(nc.semaphore(name))

        def sems(name):
            return [sem(f"{name}{layer}") for layer in range(2)]

        x_sb = sb("x_sb", [P, CT, N])
        qs = sb("q_stack", [P, N], F32R)
        ks = sb("k_stack", [P, N], F32R)
        q_now = sb("q_now", [STACK, SUB, P], F32R)
        e_t = sb("e_t", [P, E_RING, QB])
        p_hi = sb("p_hi", [P, RING, QB], F32R)
        p_lo = sb("p_lo", [P, RING, QB], F32R)
        r_all = sb("r_all", [P, QB])
        o_t = sb("o_t", [P, CT, QB])
        xs = sb("xs", [HW, QB])
        xt = sb("xt", [P, SUB, HW])
        xn = sb("xn", [P, SUB, D])
        x0n = sb("x0n", [D, QB])
        negmax = sb("negmax", [P, SUB, NCH])
        lpart = sb("lpart", [P, SUB, NCH])
        wgt = sb("wgt", [P, SUB, NCH])
        wl = sb("wl", [P, SUB, NCH])
        nm = sb("nm", [P, SUB])
        nm_cols = sb("nm_cols", [P, SUB, KROWS], F32R)
        lsum = sb("lsum", [P, SUB])
        linv = sb("linv", [P, SUB])
        r_col = sb("r_col", [P, SUB])
        l1inv = sb("l1inv", [P, SUB])
        l1r = sb("l1r", [P, SUB])
        ident = sb("ident", [P, P])
        wqk_sb = [sb("wqk_sb", [P, CT, 2 * D]), sb("wqkh_sb", [P, CT, 3 * D])]
        wv_sb = sb("wv_sb", [P, CT, C])
        wo_sb = sb("wo_sb", [D, C])
        gam = sb("gam", [P, 2])
        bqk = sb("bqk", [3 * D, 2])
        bo_sb = sb("bo_sb", [P, CT])
        gbo = sb("gbo", [P, CT])

        with ExitStack() as values:
            v_hi = values.enter_context(nc.sbuf_tensor("v_hi", [P, KT, C], F32R))
            v_lo = values.enter_context(nc.sbuf_tensor("v_lo", [P, KT, C], F32R))
        with ExitStack() as of_layer1:
            def sb1(name, shape, dt=F32):
                return of_layer1.enter_context(nc.sbuf_tensor(name, shape, dt))

            h_rows = sb1("h_rows", [D, 2, QB])
            h_st = sb1("h_st", [P, KT, HW], F32R)
            h_full = sb1("h_full", [P, len(L1_FULL), HW])
            e_full = sb1("e_full", [P, FULL_RING, QB])

        st = [bank("st0"), bank("st1")]
        mx = [bank(f"mx{i}") for i in range(3)]
        acc = [bank("acc0"), bank("acc1")]
        aux = bank("aux")
        row_banks = [mx, [*mx, acc[1]]]
        first_banks = [[aux, mx[2], mx[0], mx[1]], [*mx, aux]]

        w_in, zeroed, ident_ok, gbo_ok = sem("w_in"), sem("zeroed"), sem("ident_ok"), sem("gbo_ok")
        x_in, out_done = [sem(f"x_in{n}") for n in range(NBLK)], sem("out_done")
        qk_psum, qk_hi, qk_lo = sems("qk_psum"), sems("qk_hi"), sems("qk_lo")
        v_psum, v_hi_ok, v_ok = sems("v_psum"), sems("v_hi_ok"), sems("v_ok")
        h_rows_ok, h_turned, full_ok = sem("h_rows_ok"), sem("h_turned"), sem("full_ok")
        q_now_ok = sems("q_now_ok")
        rows_psum, rowmax_ok, rowsum_ok = sems("rows_psum"), sems("rowmax_ok"), sem("rowsum_ok")
        nm_step, nm_rowpsum, nm_rows = sems("nm_step"), sems("nm_rowpsum"), sems("nm_rows")
        wgt_ok, l_step = sem("wgt_ok"), sem("l_step")
        st_psum, exp_ok = sems("st_psum"), sems("exp_ok")
        hi_ok = [{e: sem(f"hi_{e}{n}") for e in ("act", "dve")} for n in range(2)]
        lo_ok = [{e: sem(f"lo_{e}{n}") for e in ("dve", "pool")} for n in range(2)]
        pv_done, acc0_done = sems("pv_done"), sem("acc0_done")
        r_psum, r_ok = sem("r_psum"), sem("r_ok")
        evac, y_ok = [sem("evac_c0"), sem("evac_c1")], sem("y_ok")
        xs_ok, xt_psum, xt_ok, ep_step = sem("xs_ok"), sem("xt_psum"), sem("xt_ok"), sem("ep_step")
        x0_psum, x0_ok, o_psum, o_ok = sem("x0_psum"), sem("x0_ok"), sem("o_psum"), sem("o_ok")

        block = ctx.enter_context(nc.Block())
        zeroed_all = 3

        def cols(ib, at=0, n=QB):
            return bass.ds(ib * QB + at, n)

        def e_read(eng, g, j, layer):
            kind = LO[layer][j % KT]
            if kind != "full":
                eng.wait_ge(lo_ok[layer][kind], count(LO[layer], kind, g, j))

        def take_lo(eng, kind, g, j, layer, free):
            if LO[layer][j % KT] != kind:
                return
            by = HI[layer][j % KT]
            eng.wait_ge(hi_ok[layer][by], count(HI[layer], by, g, j))
            if free:
                eng.wait_ge(pv_done[layer], PRIMED + g * KT + j + 1 - RING)
            eng.tensor_tensor(p_lo[:, j % RING, :], e_t[:, j % E_RING, :], p_hi[:, j % RING, :].bitcast(F32),
                              ALU.subtract).then_inc(lo_ok[layer][kind], 1)

        def blocks(eng, body, first_differs):
            if first_differs:
                body(0, True, False)
            with_first = 1 if first_differs else 0
            with eng.Fori(with_first, NBLK - 1) as ib:
                body(ib, False, False)
            body(NBLK - 1, False, True)

        @block.sync
        def _(eng):
            eng.sem_inc(out_done, PRIMED)

            def load(b, n):
                at = slice(n * QB, (n + 1) * QB)
                eng.dma_start(x_sb[:, :, at], x[b].rearrange("(k p) n -> p k n", p=P)[:, :, at])\
                   .then_inc(x_in[n], 16)

            def store(b, ib):
                eng.wait_ge(o_ok, PRIMED + (b * NBLK + ib) * 2 + 2)
                eng.dma_start(out[b].rearrange("(k p) n -> p k n", p=P)[:, :, cols(ib)],
                              o_t[:, :, :]).then_inc(out_done, 16)

            for sbuf, dram in ((wqk_sb[0][:, :, :], wqk), (wqk_sb[1][:, :, :], wqkh), (wv_sb[:, :, :], wv),
                               (wo_sb[:, :], wo), (gam[:, :], gamma), (bqk[:, 1:2], b_qkh),
                               (bo_sb[:, :], b_o)):
                eng.dma_start(sbuf, dram).then_inc(w_in, 16)
            for n in range(NBLK):
                load(0, n)
            for b in range(BATCH):
                for n in range(NBLK):
                    store(b, n)
                    if b < BATCH - 1:
                        load(b + 1, n)
            eng.wait_ge(out_done, PRIMED + 16 * BATCH * NBLK)

        @block.gpsimd
        def _(eng):
            eng.sem_inc(y_ok, PRIMED)
            eng.memset(ident[:, :], 0.0).then_inc(ident_ok, 1)
            eng.wait_ge(ident_ok, 1)
            eng.affine_select(out=ident[:, :], in_=ident[:, :], compare_op=ALU.not_equal, fill=1.0,
                              base=0, pattern=[[-1, P]], channel_multiplier=1).then_inc(ident_ok, 1)

            def fill(g, blk, s, layer):
                eng.wait_ge(rows_psum[layer], (g - 1) * SUB * NCH + NCH * (s + 1))
                eng.tensor_copy(q_now[:, s, :], qs[0:STACK, cols(blk, s * P, P)])\
                   .then_inc(q_now_ok[layer], 1)

            def residual(g, ib):
                for c in range(CT):
                    eng.wait_ge(evac[c], PRIMED + g + 1)
                    ins = eng.tensor_tensor(x_sb[:, c, cols(ib)], x_sb[:, c, cols(ib)], o_t[:, c, :], ALU.add)
                ins.then_inc(y_ok, 1)

            with eng.Fori(0, BATCH) as b:
                for layer in range(2):
                    g0 = b * NBLK
                    for j in range(SPLIT_AHEAD[layer]):
                        take_lo(eng, "pool", g0, j, layer, False)

                    def body(ib, fills, last):
                        g = g0 + ib
                        for j in range(KT):
                            if not last or j + SPLIT_AHEAD[layer] < KT:
                                take_lo(eng, "pool", g, j + SPLIT_AHEAD[layer], layer, True)
                            for s in range(SUB):
                                if fills and j == last_row_step(s, layer) + 1:
                                    fill(g + 2, ib + 2, s, layer)
                        if layer == 0:
                            residual(g, ib)

                    with eng.Fori(0, NBLK - 2) as ib:
                        body(ib, True, False)
                    body(NBLK - 2, False, False)
                    body(NBLK - 1, False, True)

        @block.tensor
        def _(eng):
            def project_qk(b, g0, n, k, layer):
                to = st[n % 2][0:(2 + layer) * D, :]
                if k == 0:
                    if layer == 0:
                        eng.wait_ge(x_in[n], 16 * (b + 1))
                    else:
                        eng.wait_ge(y_ok, PRIMED + g0 + n + 1)
                    if n > 1:
                        eng.wait_ge(qk_lo[layer], LO_STEPS[layer] * (g0 + n - 1))
                mm = eng.matmul(to, wqk_sb[layer][:, k, :], x_sb[:, k, n * QB:(n + 1) * QB],
                                start=(k == 0), stop=(k == 1))
                if k == 1:
                    mm.then_inc(qk_psum[layer], 1)

            def project_v(g0, t):
                pair, i = divmod(t, 2)
                if pair >= 2 and i == 0:
                    eng.wait_ge(v_ok[0], 2 * g0 + pair - 1)
                for k in range(CT):
                    mm = eng.matmul(acc[pair % 2][:, i * C:(i + 1) * C], x_sb[:, k, t * P:(t + 1) * P],
                                    wv_sb[:, k, :], start=(i == 0 and k == 0), stop=(i == 1 and k == 1),
                                    skip_group_check=True)
                if i == 1:
                    mm.then_inc(v_psum[0], 1)

            def turn_h(g0, t):
                half, i = divmod(t, KT // 2)
                n, s = divmod(t, SUB)
                mm = eng.transpose(acc[half][:, i * D:(i + 1) * D], h_rows[:, n % 2, s * P:(s + 1) * P],
                                   ident[0:D, 0:D])
                if s == SUB - 1:
                    mm.then_inc(h_turned, 1)

            def row_tile(g, u, s, c, layer, to, wait_for):
                if wait_for is not None:
                    used = rowsum_ok if layer == 0 else rowmax_ok[1]
                    eng.wait_ge(used, g * SUB * NCH + wait_for + 1)
                eng.matmul(to[:, :], q_now[:, s, :], ks[0:STACK, c * CHUNK:(c + 1) * CHUNK],
                           start=True, stop=True).then_inc(rows_psum[layer], 1)

            def rows(g, u, layer):
                turns = NMX[layer]
                same_bank = [v for v in range(-SUB * NCH, 0) if v % (SUB * NCH) % turns == u]
                before = u - turns if u >= turns else same_bank[-1]
                row_tile(g, u, u // NCH, u % NCH, layer, row_banks[layer][u % turns], before)

            def first_row(g, c, s, layer):
                if s == 0:
                    eng.wait_ge(qk_lo[layer], LO_STEPS[layer] * (g + c + 1))
                    if c == 0:
                        eng.wait_ge(q_now_ok[layer], g * SUB + SUB)
                u, turns = SUB * c + s, SUB
                row_tile(g, u, s, c, layer, first_banks[layer][u % turns], u - turns if u >= turns else None)

            def max_rows(g, s, layer, groups):
                eng.wait_ge(nm_step[layer], 3 * (g * SUB + groups))
                return eng.transpose(aux[0:KROWS, s * P:(s + 1) * P], nm_cols[:, s, :].bitcast(F32),
                                     ident[:, :])

            def factor_rows(g):
                eng.wait_ge(l_step, 4 * (g * SUB + SUB))
                for s in range(SUB):
                    mm = eng.transpose(aux[:, s * P:(s + 1) * P], r_col[:, s:s + 1].to_broadcast([P, P]),
                                       ident[:, :])
                mm.then_inc(r_psum, 1)

            def scores_t(g, ib, j, layer, free):
                if j % KT == 0:
                    eng.wait_ge(nm_rows[layer], (g + j // KT) * SUB + SUB)
                if free:
                    eng.wait_ge(exp_ok[layer], g * KT + j - 1)
                eng.matmul(st[j % 2][:, :], ks[0:KROWS, (j % KT) * P:(j % KT + 1) * P],
                           qs[0:KROWS, cols(ib + j // KT)], start=True, stop=True).then_inc(st_psum[layer], 1)

            def sums0(g, j):
                eng.wait_ge(lo_ok[0][LO[0][j]], count(LO[0], LO[0][j], g, j))
                for t, c in PV_ORDER.get(j, ((j, 0), (j, 1))):
                    a, b = p_hi[:, t % RING, :], p_lo[:, t % RING, :]
                    hi, lo = v_hi[:, t, c * P:(c + 1) * P], v_lo[:, t, c * P:(c + 1) * P]
                    if t == 0:
                        eng.wait_ge(evac[c], PRIMED + g)
                    eng.matmul(acc[c][:, :], hi, a, start=(t == 0), stop=False)
                    eng.matmul(acc[c][:, :], lo, a, start=False, stop=False)
                    mm = eng.matmul(acc[c][:, :], hi, b, start=False, stop=(t == KT - 1))
                    if c == 1:
                        mm.then_inc(pv_done[0], 1)
                    elif t == KT - 1:
                        mm.then_inc(acc0_done, 1)

            def sums1(g, j):
                kind = LO[1][j]
                if kind == "full":
                    eng.wait_ge(exp_ok[1], g * KT + j + 1)
                else:
                    eng.wait_ge(lo_ok[1][kind], count(LO[1], kind, g, j))
                if j == 0:
                    eng.wait_ge(xs_ok, PRIMED + g)
                if kind == "full":
                    terms = [(h_full[:, L1_FULL.index(j), :], e_full[:, L1_FULL.index(j) % FULL_RING, :])]
                else:
                    terms = [(h_st[:, j, :], p[:, j % RING, :]) for p in (p_hi, p_lo)]
                for n, (h, p) in enumerate(terms):
                    mm = eng.matmul(acc[0][0:HW, :], h, p, start=(j == 0 and n == 0),
                                    stop=(j == KT - 1 and n == len(terms) - 1))
                mm.then_inc(pv_done[1], 1)

            def turn_sums(g):
                eng.wait_ge(xs_ok, PRIMED + g + 1)
                for s in range(SUB):
                    mm = eng.transpose(aux[:, s * HW:(s + 1) * HW], xs[:, s * P:(s + 1) * P],
                                       ident[0:HW, 0:HW])
                mm.then_inc(xt_psum, 1)

            def turn_back(g):
                eng.wait_ge(ep_step, 4 * g + 4)
                for s in range(SUB):
                    mm = eng.transpose(aux[0:D, s * P:(s + 1) * P], xn[:, s, :], ident[:, :])
                mm.then_inc(x0_psum, 1)

            def widen(g, c, to):
                if c == 0:
                    eng.wait_ge(x0_ok, g + 1)
                eng.matmul(to[:, :], wo_sb[:, c * P:(c + 1) * P], x0n[:, :], start=True, stop=True)\
                   .then_inc(o_psum, 1)

            for done in pv_done:
                eng.sem_inc(done, PRIMED)
            eng.wait_ge(w_in, 16 * 7)
            eng.wait_ge(ident_ok, 2)
            eng.wait_ge(zeroed, zeroed_all)
            with eng.Fori(0, BATCH) as b:
                for layer in range(2):
                    g0 = b * NBLK
                    for k in range(CT):
                        project_qk(b, g0, 0, k, layer)
                    for n in range(NBLK):
                        for s in range(SUB):
                            t = SUB * n + s
                            if layer == 0:
                                if t == 2:
                                    eng.wait_ge(o_ok, PRIMED + 2 * g0)
                                project_v(g0, t)
                            elif s == 1 and n:
                                if (n - 1) % (NBLK // 2) == 0:
                                    eng.wait_ge(evac[2 * (n - 1) // NBLK], PRIMED + g0 + NBLK)
                                eng.wait_ge(h_rows_ok, g0 + n)
                            if n:
                                first_row(g0, n - 1, s, layer)
                            if s in QK_AT[layer] and n < NBLK - 1:
                                project_qk(b, g0, n + 1, QK_AT[layer].index(s), layer)
                            if layer == 1 and s >= 2 and n:
                                for i in range(2):
                                    turn_h(g0, SUB * (n - 1) + 2 * (s - 2) + i)
                    if layer == 1:
                        eng.wait_ge(h_rows_ok, g0 + NBLK)
                    for s in range(SUB):
                        first_row(g0, NBLK - 1, s, layer)
                        if layer == 1:
                            turn_h(g0, SUB * (NBLK - 1) + s)
                    if layer == 0:
                        eng.wait_ge(rowsum_ok, (g0 + 1) * SUB * NCH - 3)
                    for s in range(SUB):
                        mm = max_rows(g0, s, layer, SUB)
                    mm.then_inc(nm_rowpsum[layer], SUB)
                    for j in range(AHEAD[layer]):
                        if j == AHEAD[layer] - 1:
                            eng.wait_ge(v_ok[layer], 2 * g0 + 2 * NBLK if layer == 0 else 2 * b + 2)
                            if layer == 1:
                                eng.wait_ge(full_ok, (len(L1_FULL) + 3) * (b + 1))
                        scores_t(g0, 0, j, layer, j >= 2)

                    def body(ib, first, last):
                        g = g0 + ib
                        for j in range(KT):
                            if not last or j + AHEAD[layer] < KT:
                                scores_t(g, ib, j + AHEAD[layer], layer, True)
                            if not last:
                                for u in row_tiles(j, layer):
                                    if u % NCH == 0:
                                        eng.wait_ge(q_now_ok[layer], (g + 1) * SUB + u // NCH + 1)
                                    rows(g + 1, u, layer)
                                for s in range(SUB):
                                    if j == last_row_step(s, layer) + LATE[layer]:
                                        if s:
                                            eng.wait_ge(nm_rows[layer], (g + 1) * SUB + s)
                                        elif layer == 0:
                                            eng.wait_ge(r_ok, PRIMED + g + 1)
                                        elif not first:
                                            eng.wait_ge(x0_ok, g)
                                        if layer == 1 and s == 1 and not first:
                                            eng.wait_ge(o_ok, PRIMED + 2 * g)
                                        max_rows(g + 1, s, layer, s + 1).then_inc(nm_rowpsum[layer], 1)
                            if layer == 0:
                                if j == 2:
                                    factor_rows(g)
                                sums0(g, j)
                            else:
                                if not first and j == TURN_SUMS:
                                    turn_sums(g - 1)
                                if not first and j == TURN_BACK:
                                    turn_back(g - 1)
                                if not first and j == WIDEN[0]:
                                    if not last:
                                        eng.wait_ge(nm_rows[1], (g + 1) * SUB + 1)
                                    widen(g - 1, 0, aux)
                                if not first and j == WIDEN[1]:
                                    eng.wait_ge(o_ok, PRIMED + 2 * g - 1)
                                    widen(g - 1, 1, aux)
                                sums1(g, j)

                    blocks(eng, body, layer == 1)
                    if layer == 1:
                        turn_sums(g0 + NBLK - 1)
                        turn_back(g0 + NBLK - 1)
                        for c, to in enumerate((acc[1], aux)):
                            widen(g0 + NBLK - 1, c, to)

        @block.scalar
        def _(eng):
            def stack_hi(g0, n, layer):
                for r, (to, places) in enumerate(((qs, (0, 2)), (ks, (0, 1)))):
                    for i, at in enumerate(places if COPY_HI[layer] == "act" else places[:1]):
                        if i == 0 and r == 0:
                            eng.wait_ge(qk_psum[layer], g0 + n + 1)
                        eng.activation(to[at * D:(at + 1) * D, n * QB:(n + 1) * QB],
                                       st[n % 2][r * D:(r + 1) * D, :], ACT.Identity,
                                       bias=bqk[r * D:(r + 1) * D, layer:layer + 1]).then_inc(qk_hi[layer], 1)

            def take_h(g0, n):
                if n >= 2:
                    eng.wait_ge(h_turned, g0 + n - 1)
                eng.activation(h_rows[:, n % 2, :], st[n % 2][2 * D:3 * D, :], ACT.Identity,
                               bias=bqk[2 * D:3 * D, 1:2]).then_inc(h_rows_ok, 1)

            def first_queries(g, blk, layer):
                if blk == 0:
                    eng.wait_ge(qk_lo[layer], LO_STEPS[layer] * g + LO_STEPS[layer] // 2)
                else:
                    eng.wait_ge(rows_psum[layer], (g + 1) * SUB * NCH)
                eng.activation(q_now[:, :, :], qs[0:STACK, blk * QB:(blk + 1) * QB].bitcast(F32), ACT.Copy)\
                   .then_inc(q_now_ok[layer], SUB)

            def rowsum(g, u, s, c, of):
                eng.wait_ge(rowmax_ok[0], g * SUB * NCH + u + 1)
                scores = of[u % len(of)][:, :]
                eng.activation(scores, scores, ACT.Exp, bias=negmax[:, s, c:c + 1],
                               accum_out=lpart[:, s, c:c + 1]).then_inc(rowsum_ok, 1)

            def weights(g, s, first):
                eng.wait_ge(nm_step[0], 3 * g * SUB + (SUB if first else 3 * s + 1))
                eng.activation(wgt[:, s, :], negmax[:, s, :], ACT.Exp, scale=-1.0,
                               bias=nm[:, s:s + 1]).then_inc(wgt_ok, 1)

            def put_max_rows(g, blk, s, n, layer):
                eng.wait_ge(nm_rowpsum[layer], g * SUB + s + n)
                eng.activation(qs[MAXROW:KROWS, cols(blk, s * P, n * P)],
                               aux[MAXROW:KROWS, s * P:(s + n) * P], ACT.Copy).then_inc(nm_rows[layer], n)

            def exps(g, j, layer, free):
                eng.wait_ge(st_psum[layer], g * KT + j + 1)
                to = e_t[:, j % E_RING, :]
                if LO[layer][j % KT] == "full":
                    i = L1_FULL.index(j)
                    if i >= FULL_RING:
                        eng.wait_ge(pv_done[1], PRIMED + g * KT + L1_FULL[i - FULL_RING] + 1)
                    to = e_full[:, i % FULL_RING, :]
                elif free:
                    e_read(eng, g, j - E_RING, layer)
                eng.activation(to, st[j % 2][:, :], ACT.Exp).then_inc(exp_ok[layer], 1)

            def hi(g, j, layer, free):
                if HI[layer][j % KT] != "act":
                    return
                eng.wait_ge(exp_ok[layer], g * KT + j + 1)
                if free:
                    eng.wait_ge(pv_done[layer], PRIMED + g * KT + j + 1 - RING)
                eng.activation(p_hi[:, j % RING, :], e_t[:, j % E_RING, :], ACT.Copy)\
                   .then_inc(hi_ok[layer]["act"], 1)

            def put_factors(g):
                eng.wait_ge(r_psum, g + 1)
                eng.wait_ge(evac[1], PRIMED + g)
                eng.activation(r_all[:, :], aux[:, :], ACT.Copy).then_inc(r_ok, 1)

            def h_hi(b, half):
                t = slice(half * KT // 2, (half + 1) * KT // 2)
                eng.wait_ge(h_turned, b * NBLK + (half + 1) * NBLK // 2)
                eng.activation(h_st[:, t, 0:D], acc[half][:, :], ACT.Copy).then_inc(v_hi_ok[1], 1)

            for done in (r_ok, xs_ok):
                eng.sem_inc(done, PRIMED)
            eng.wait_ge(w_in, 16 * 7)
            eng.wait_ge(zeroed, zeroed_all)
            with eng.Fori(0, BATCH) as b:
                for layer in range(2):
                    g0 = b * NBLK
                    stack_hi(g0, 0, layer)
                    if layer == 1:
                        take_h(g0, 0)
                    first_queries(g0, 0, layer)
                    for n in range(NBLK):
                        for s in range(SUB):
                            if layer == 0 and s % 2 == 1:
                                pair = 2 * n + s // 2
                                eng.wait_ge(v_psum[0], 2 * g0 + pair + 1)
                                eng.activation(v_hi[:, 2 * pair:2 * pair + 2, :], acc[pair % 2][:, :],
                                               ACT.Copy).then_inc(v_hi_ok[0], 1)
                            u = SUB * (n - 1) + s - 1
                            if layer == 0 and u >= 0:
                                rowsum(g0, u, u % SUB, u // SUB, first_banks[0])
                            if s == 2 and n < NBLK - 1:
                                stack_hi(g0, n + 1, layer)
                                if layer == 1:
                                    take_h(g0, n + 1)
                        if layer == 1 and n == NBLK - 1:
                            h_hi(b, 0)
                    if layer == 0:
                        for u in range(SUB * (NBLK - 1) - 1, SUB * NBLK):
                            rowsum(g0, u, u % SUB, u // SUB, first_banks[0])
                    if layer == 1:
                        h_hi(b, 1)
                    put_max_rows(g0, 0, 0, SUB, layer)
                    for j in range(AHEAD[layer]):
                        exps(g0, j, layer, j >= E_RING)
                        if j == 1:
                            first_queries(g0, 1, layer)
                            if layer == 0:
                                for s in range(SUB):
                                    weights(g0, s, True)
                        if j >= AHEAD[layer] - SPLIT_AHEAD[layer]:
                            hi(g0, j - AHEAD[layer] + SPLIT_AHEAD[layer], layer, False)

                    def body(ib, first, last):
                        g = g0 + ib
                        for j in range(KT):
                            if not last or j + AHEAD[layer] < KT:
                                exps(g, j + AHEAD[layer], layer, True)
                            if not last or j + SPLIT_AHEAD[layer] < KT:
                                hi(g, j + SPLIT_AHEAD[layer], layer, True)
                            if not last:
                                if layer == 0:
                                    for u in row_tiles(j, layer):
                                        rowsum(g + 1, u, u // NCH, u % NCH, row_banks[0])
                                        if u % NCH == NCH - 1:
                                            weights(g + 1, u // NCH, False)
                                for s in range(SUB):
                                    if j == last_row_step(s, layer) + LATE[layer]:
                                        put_max_rows(g + 1, ib + 1, s, 1, layer)
                            if layer == 0 and j == 3:
                                put_factors(g)
                            if layer == 1 and not first and j == TAKE_TURNED:
                                take_turned(g - 1)
                            if layer == 1 and not first and j == TAKE_BACK:
                                take_back(g - 1)
                        if layer == 1:
                            eng.wait_ge(pv_done[1], PRIMED + g * KT + KT)
                            eng.activation(xs[:, :], acc[0][0:HW, :], ACT.Copy).then_inc(xs_ok, 1)

                    def take_turned(g):
                        eng.wait_ge(xt_psum, g + 1)
                        eng.activation(xt[:, :, :], aux[:, 0:SUB * HW], ACT.Copy).then_inc(xt_ok, 1)

                    def take_back(g):
                        eng.wait_ge(x0_psum, g + 1)
                        eng.activation(x0n[:, :], aux[0:D, :], ACT.Copy).then_inc(x0_ok, 1)

                    blocks(eng, body, layer == 1)
                    if layer == 1:
                        take_turned(g0 + NBLK - 1)
                        take_back(g0 + NBLK - 1)

        @block.vector
        def _(eng):
            def stack_lo(g0, n, r, layer):
                to, lo, copy = ((qs, 1, 2), (ks, 2, 1))[r]
                cut, steps, here = slice(n * QB, (n + 1) * QB), HI_STEPS[layer], slice(r * D, (r + 1) * D)
                eng.wait_ge(qk_hi[layer], steps * (g0 + n) + steps // 2 * (r + 1))
                eng.scalar_tensor_tensor(to[lo * D:(lo + 1) * D, cut], st[n % 2][here, :],
                                         bqk[here, layer:layer + 1], to[0:D, cut].bitcast(F32),
                                         ALU.add, ALU.subtract).then_inc(qk_lo[layer], 1)
                if COPY_HI[layer] == "dve":
                    eng.tensor_copy(to[copy * D:(copy + 1) * D, cut], to[0:D, cut].bitcast(F32))\
                       .then_inc(qk_lo[layer], 1)

            def rowmax(g, u, s, c, layer, of):
                eng.wait_ge(rows_psum[layer], g * SUB * NCH + u + 1)
                eng.tensor_reduce(negmax[:, s, c:c + 1], of[u % len(of)][:, :], AX.X, ALU.max, negate=True)\
                   .then_inc(rowmax_ok[layer], 1)

            def maximum(g, s, n, parts, layer):
                to, done = slice(s, s + n), 3 * (g * SUB + s)
                eng.wait_ge(rowmax_ok[layer], g * SUB * NCH + parts)
                eng.tensor_reduce(nm[:, to], negmax[:, to, :], AX.X, ALU.min).then_inc(nm_step[layer], n)
                eng.wait_ge(nm_step[layer], done + n)
                whole = nm[:, to].rearrange("p (s a) -> p s a", a=1)
                hi, lo = nm_cols[:, to, MAXROW:MAXROW + 1], nm_cols[:, to, MAXROW + 1:KROWS]
                eng.tensor_copy(hi, whole).then_inc(nm_step[layer], n)
                eng.wait_ge(nm_step[layer], done + 2 * n)
                eng.tensor_tensor(lo, whole, hi.bitcast(F32), ALU.subtract).then_inc(nm_step[layer], n)

            def factor(g, s, n, free):
                to, done = slice(s, s + n), 4 * (g * SUB + s)
                eng.wait_ge(wgt_ok, g * SUB + s + n)
                eng.tensor_tensor(wl[:, to, :], wgt[:, to, :], lpart[:, to, :], ALU.mult).then_inc(l_step, n)
                eng.wait_ge(l_step, done + n)
                eng.tensor_reduce(lsum[:, to], wl[:, to, :], AX.X, ALU.add).then_inc(l_step, n)
                eng.wait_ge(l_step, done + 2 * n)
                eng.reciprocal(linv[:, to], lsum[:, to]).then_inc(l_step, n)
                eng.wait_ge(l_step, done + 3 * n)
                if free:
                    eng.wait_ge(r_psum, g)
                eng.tensor_scalar(r_col[:, to], linv[:, to], gam[:, 0:1], None, ALU.mult)\
                   .then_inc(l_step, n)

            def split(g, j, layer, free):
                if HI[layer][j % KT] == "dve":
                    eng.wait_ge(exp_ok[layer], g * KT + j + 1)
                    if free:
                        eng.wait_ge(pv_done[layer], PRIMED + g * KT + j + 1 - RING)
                    eng.tensor_copy(p_hi[:, j % RING, :], e_t[:, j % E_RING, :])\
                       .then_inc(hi_ok[layer]["dve"], 1)
                take_lo(eng, "dve", g, j, layer, free)

            def take_sums(g):
                eng.wait_ge(r_ok, PRIMED + g + 1)
                for c in range(CT):
                    if c == 0:
                        eng.wait_ge(acc0_done, g + 1)
                        eng.wait_ge(y_ok, PRIMED + g)
                    else:
                        eng.wait_ge(pv_done[0], PRIMED + g * KT + KT)
                    eng.tensor_tensor(o_t[:, c, :], acc[c][:, :], r_all[:, :], ALU.mult).then_inc(evac[c], 1)

            def normalise(g):
                eng.wait_ge(xt_ok, g + 1)
                eng.reciprocal(l1inv[:, :], xt[:, :, 2 * D:HW]).then_inc(ep_step, 1)
                eng.tensor_tensor(xt[:, :, 0:D], xt[:, :, 0:D], xt[:, :, D:2 * D], ALU.add)\
                   .then_inc(ep_step, 1)
                eng.wait_ge(ep_step, 4 * g + 2)
                eng.tensor_scalar(l1r[:, :], l1inv[:, :], gam[:, 1:2], None, ALU.mult).then_inc(ep_step, 1)
                eng.wait_ge(ep_step, 4 * g + 3)
                eng.tensor_tensor(xn[:, :, :], xt[:, :, 0:D],
                                  l1r[:, :].rearrange("p (s a) -> p s a", a=1).to_broadcast([P, SUB, D]),
                                  ALU.mult).then_inc(ep_step, 1)

            def finish(g, ib, c, at):
                if c == 0:
                    eng.wait_ge(out_done, PRIMED + 16 * g)
                eng.wait_ge(o_psum, 2 * g + c + 1)
                eng.scalar_tensor_tensor(o_t[:, c, :], at[:, :], gbo[:, c:c + 1], x_sb[:, c, cols(ib)],
                                         ALU.add, ALU.add).then_inc(o_ok, 1)

            def h_ones():
                eng.memset(h_st[:, :, 2 * D:HW].bitcast(F32), 1.0).then_inc(full_ok, 1)
                eng.memset(h_full[:, :, D:2 * D], 0.0).then_inc(full_ok, 1)
                eng.memset(h_full[:, :, 2 * D:HW], 1.0).then_inc(full_ok, 1)

            def h_lo(b, half):
                t = slice(half * KT // 2, (half + 1) * KT // 2)
                whole = acc[half][:, :].rearrange("p (t d) -> p t d", d=D)
                eng.wait_ge(v_hi_ok[1], 2 * b + half + 1)
                eng.tensor_tensor(h_st[:, t, D:2 * D], whole, h_st[:, t, 0:D].bitcast(F32),
                                  ALU.subtract).then_inc(v_ok[1], 1)
                for i, tile in enumerate(L1_FULL):
                    if tile // (KT // 2) == half:
                        eng.tensor_copy(h_full[:, i, 0:D], whole[:, tile % (KT // 2), :]).then_inc(full_ok, 1)

            def values_lo(g0, pair):
                t = slice(2 * pair, 2 * pair + 2)
                eng.wait_ge(v_hi_ok[0], 2 * g0 + pair + 1)
                eng.tensor_tensor(v_lo[:, t, :], acc[pair % 2][:, :].rearrange("p (t c) -> p t c", t=2),
                                  v_hi[:, t, :].bitcast(F32), ALU.subtract).then_inc(v_ok[0], 1)

            for done in (*evac, o_ok):
                eng.sem_inc(done, PRIMED)
            eng.memset(bqk[:, 0:1], 0.0).then_inc(zeroed, 1)
            eng.memset(ks[MAXROW:KROWS, :].bitcast(F32), 1.0).then_inc(zeroed, 1)
            eng.memset(nm_cols[:, :, :].bitcast(F32), 0.0).then_inc(zeroed, 1)
            eng.wait_ge(w_in, 16 * 7)
            eng.wait_ge(zeroed, zeroed_all)
            eng.tensor_scalar(gbo[:, :], bo_sb[:, :], gam[:, 1:2], None, ALU.mult).then_inc(gbo_ok, 1)
            eng.wait_ge(gbo_ok, 1)
            with eng.Fori(0, BATCH) as b:
                for layer in range(2):
                    g0 = b * NBLK
                    if layer == 1:
                        h_ones()
                    for n in range(NBLK):
                        for s in range(SUB):
                            if layer == 0 and s < 2:
                                stack_lo(g0, n, s, layer)
                            if n:
                                rowmax(g0, SUB * (n - 1) + s, s, n - 1, layer, first_banks[layer])
                            if layer == 1 and s < 2:
                                stack_lo(g0, n, s, layer)
                            if layer == 0 and s % 2 == 0 and 2 * n + s // 2 > 0:
                                values_lo(g0, 2 * n + s // 2 - 1)
                    for s in range(SUB):
                        rowmax(g0, SUB * (NBLK - 1) + s, s, NBLK - 1, layer, first_banks[layer])
                    maximum(g0, 0, SUB, SUB * NCH, layer)
                    if layer == 0:
                        values_lo(g0, 2 * NBLK - 1)
                        factor(g0, 0, SUB, False)
                    else:
                        h_lo(b, 0)
                        h_lo(b, 1)
                    for j in range(SPLIT_AHEAD[layer]):
                        split(g0, j, layer, False)

                    def body(ib, first, last):
                        g = g0 + ib
                        for j in range(KT):
                            if not last:
                                for u in row_tiles(j, layer):
                                    s, c = divmod(u, NCH)
                                    rowmax(g + 1, u, s, c, layer, row_banks[layer])
                                    if c == NCH - 1:
                                        maximum(g + 1, s, 1, u + 1, layer)
                                if layer == 0:
                                    for s in range(SUB):
                                        if j == last_row_step(s, layer) + LATE[layer]:
                                            factor(g + 1, s, 1, True)
                            if layer == 0 and j == KT - 1:
                                take_sums(g)
                            if not last or j + SPLIT_AHEAD[layer] < KT:
                                split(g, j + SPLIT_AHEAD[layer], layer, True)
                            if layer == 1 and not first and j == NORMALISE:
                                normalise(g - 1)
                            if layer == 1 and not first and j in FINISH:
                                finish(g - 1, ib - 1, FINISH.index(j), aux)

                    blocks(eng, body, layer == 1)
                    if layer == 1:
                        normalise(g0 + NBLK - 1)
                        for c, at in enumerate((acc[1], aux)):
                            finish(g0 + NBLK - 1, NBLK - 1, c, at)


def kernel(x, L0_conv_q_weight, L0_conv_k_weight, L0_conv_v_weight, L0_conv_gamma,
           L1_conv_wf, L1_conv_bf, L1_conv_wg, L1_conv_bg, L1_conv_wh, L1_conv_bh,
           L1_conv_wv, L1_conv_bv, L1_conv_gamma):
    import numpy as np
    from concourse import bacc
    from concourse.bass_utils import run_bass_kernel_spmd

    x = np.asarray(x)
    by_channel = lambda *ws: np.concatenate([np.asarray(w).T.reshape(CT, P, -1) for w in ws], axis=2)\
        .transpose(1, 0, 2)
    row = lambda v: np.broadcast_to(np.asarray(v), (P, np.asarray(v).size))
    arrays = {
        "x": x.reshape(BATCH, C, N),
        "wqk": by_channel(L0_conv_q_weight, L0_conv_k_weight),
        "wqkh": by_channel(L1_conv_wf, L1_conv_wg, L1_conv_wh),
        "wv": by_channel(L0_conv_v_weight),
        "wo": np.asarray(L1_conv_wv).T,
        "gamma": np.concatenate([row(L0_conv_gamma), row(L1_conv_gamma)], axis=1),
        "b_qkh": np.concatenate([np.asarray(v) for v in (L1_conv_bf, L1_conv_bg, L1_conv_bh)])[:, None],
        "b_o": np.asarray(L1_conv_bv).reshape(CT, P).T,
    }
    arrays = {f"in_{n}": np.ascontiguousarray(a) for n, a in arrays.items()}
    nc = bacc.Bacc("TRN2", target_bir_lowering=False, num_devices=1)
    args = [nc.dram_tensor(n, a.shape, mybir.dt.from_np(a.dtype), kind="ExternalInput").ap()
            for n, a in arrays.items()]
    out = nc.dram_tensor("out", (BATCH, C, N), F32, kind="ExternalOutput").ap()
    build(nc, *args, out)
    r = run_bass_kernel_spmd(nc, [arrays], core_ids=[0])
    return r.results[0]["out"].reshape(x.shape)
```
